# Optimizing a Trainium2 kernel written in Bass

```python
import numpy as np
import jax
import jax.numpy as jnp

def _softmax(x, axis=-1):
    return jax.nn.softmax(x, axis=axis)

def _gelu(x):
    return jax.nn.gelu(x, approximate=True)

def _silu(x):
    return jax.nn.silu(x)

def _sigmoid(x):
    return jax.nn.sigmoid(x)

def _layernorm(x, axis=-1, eps=1e-05):
    m = jnp.mean(x, axis=axis, keepdims=True)
    v = jnp.var(x, axis=axis, keepdims=True)
    return (x - m) / jnp.sqrt(v + eps)

def _scatter_add(tgt, idx, src, axis=0):
    return tgt.at[idx].add(src)

def _segment_sum(src, seg, n):
    return jax.ops.segment_sum(src, seg, n)
kernel_name = 'mk_adaln_d1_jaxref_r8_b5e2ff'

def setup_inputs(seed: int=0):
    np.random.seed(seed)
    _w = jnp.asarray

    def _L0_attn_setup():
        import jax, jax.numpy as jnp
        import numpy as np
        N_HEADS = 16
        PALACE_PERIOD = 8

        def _palace_mask(T, inter_palace_weight):
            idx = jnp.arange(T) % PALACE_PERIOD
            intra = idx[:, None] == idx[None, :]
            w = jax.nn.sigmoid(inter_palace_weight)
            return jnp.where(intra, jnp.float32(1.0), w)
        key = jax.random.key(seed)
        B, T, D = (2, 256, 128)
        x = jax.random.normal(key, (B, T, D), dtype=jnp.float32)
        inter_palace_weight = jnp.array(0.1, dtype=jnp.float32)
        return {'x': x, 'inter_palace_weight': inter_palace_weight}
    _L0_attn_in = _L0_attn_setup()

    def _L0_ffn_setup():
        import jax, jax.numpy as jnp
        import numpy as np
        HIDDEN = 128
        NUM_EXPERTS = 16
        TOP_K = 6
        EPS = 1e-10
        key = jax.random.key(seed)
        k1, k2, k3, k4 = jax.random.split(key, 4)
        tokens = jax.random.normal(k1, (4, 256, HIDDEN), dtype=jnp.float32)
        bound = 1.0 / np.sqrt(HIDDEN)
        router_w = jax.random.uniform(k2, (NUM_EXPERTS, HIDDEN), jnp.float32, -bound, bound)
        router_b = jax.random.uniform(k3, (NUM_EXPERTS,), jnp.float32, -bound, bound)
        expert_w = jax.random.normal(k4, (NUM_EXPERTS, HIDDEN, HIDDEN), dtype=jnp.float32) / np.sqrt(HIDDEN)
        return {'tokens': tokens, 'router_w': router_w, 'router_b': router_b, 'expert_w': expert_w}
    _L0_ffn_in = _L0_ffn_setup()
    _L0_c = _w((lambda *s: np.random.randn(*s).astype(np.float32) * 0.05)(8, 128))
    _L0_wmod = _w((lambda *s: np.random.randn(*s).astype(np.float32) * 0.05)(128, 6 * 128) * 128 ** (-0.5))
    _d = {'L0_attn_x': _L0_attn_in['x'], 'L0_attn_inter_palace_weight': _L0_attn_in['inter_palace_weight'], 'L0_ffn_router_w': _L0_ffn_in['router_w'], 'L0_ffn_router_b': _L0_ffn_in['router_b'], 'L0_ffn_expert_w': _L0_ffn_in['expert_w'], 'L0_c': _L0_c, 'L0_wmod': _L0_wmod}
    _x0 = _d['L0_attn_x']
    _d['L0_attn_x'] = jax.random.normal(jax.random.fold_in(jax.random.key(seed), 1), (8, 512, 128), dtype=_x0.dtype)
    del _x0
    return _d

def reference(L0_attn_x, L0_attn_inter_palace_weight, L0_ffn_router_w, L0_ffn_router_b, L0_ffn_expert_w, L0_c, L0_wmod):

    def _L0_attn_ref(x, inter_palace_weight):
        import jax, jax.numpy as jnp
        import numpy as np
        N_HEADS = 16
        PALACE_PERIOD = 8

        def _palace_mask(T, inter_palace_weight):
            idx = jnp.arange(T) % PALACE_PERIOD
            intra = idx[:, None] == idx[None, :]
            w = jax.nn.sigmoid(inter_palace_weight)
            return jnp.where(intra, jnp.float32(1.0), w)
        B, T, D = x.shape
        H = N_HEADS
        hd = D // H
        scale = hd ** (-0.5)
        q = x.reshape(B, T, H, hd).transpose(0, 2, 1, 3)
        scores = jnp.einsum('bhqd,bhkd->bhqk', q, q) * scale
        m = _palace_mask(T, inter_palace_weight)
        attn = jax.nn.softmax(scores * m, axis=-1)
        out = jnp.einsum('bhqk,bhkd->bhqd', attn, q)
        return out.transpose(0, 2, 1, 3).reshape(B, T, D)

    def _L0_ffn_ref(tokens, router_w, router_b, expert_w):
        import jax, jax.numpy as jnp
        import numpy as np
        HIDDEN = 128
        NUM_EXPERTS = 16
        TOP_K = 6
        EPS = 1e-10
        B, S, H = tokens.shape
        E = expert_w.shape[0]
        T = B * S
        logits = jnp.einsum('bsh,eh->bse', tokens, router_w) + router_b
        probs = jax.nn.softmax(logits, axis=-1)
        top_p, top_i = jax.lax.top_k(probs, TOP_K)
        top_p = top_p / (jnp.sum(top_p, axis=-1, keepdims=True) + EPS)
        x = tokens.reshape(T, H)
        flat_i = top_i.reshape(T, TOP_K)
        flat_p = top_p.reshape(T, TOP_K)
        gate = jnp.zeros((T, E), dtype=flat_p.dtype)
        gate = gate.at[jnp.arange(T)[:, None], flat_i].add(flat_p)
        acc = jnp.maximum(jnp.sum(gate, axis=-1), EPS)
        out = jnp.zeros_like(x)
        for e in range(E):
            out = out + x @ expert_w[e] * gate[:, e:e + 1]
        out = (out / acc[:, None]).reshape(B, S, H)
        out = out + EPS * jnp.sum(top_p, axis=-1, keepdims=True)
        return out
    x = L0_attn_x
    mod = (_silu(L0_c) @ L0_wmod).reshape(L0_c.shape[0], 6, 1, -1)
    sa, ca, ga, sb, cb, gb = (mod[:, 0], mod[:, 1], mod[:, 2], mod[:, 3], mod[:, 4], mod[:, 5])
    ga = (2 * (ga >= 0) - 1) * jnp.maximum(jnp.abs(ga), 0.25)
    gb = (2 * (gb >= 0) - 1) * jnp.maximum(jnp.abs(gb), 0.25)
    h = _layernorm(x, axis=-1) * (1 + ca) + sa
    x = x + ga * _L0_attn_ref(h, L0_attn_inter_palace_weight)
    h = _layernorm(x, axis=-1) * (1 + cb) + sb
    x = x + gb * _L0_ffn_ref(h, L0_ffn_router_w, L0_ffn_router_b, L0_ffn_expert_w)
    return x

_drawn_inputs = setup_inputs


def setup_inputs(seed=0):
    import zlib

    import numpy as np

    out = dict(_drawn_inputs(seed))
    spreads = {}
    factors = {'L0_ffn_router_b': 3.039}
    for name, (base, spread) in spreads.items():
        noise = np.random.default_rng([zlib.crc32(name.encode()), seed]).standard_normal(out[name].shape)
        drawn = base * np.exp(spread * noise) if base else spread * noise
        out[name] = jnp.asarray(drawn.astype(out[name].dtype))
    for name, factor in factors.items():
        out[name] = (out[name] * factor).astype(out[name].dtype)
    return out
```

```python
from contextlib import ExitStack

import numpy as np
import concourse.bass as bass
from concourse import mybir

F32 = mybir.dt.float32
BF16 = mybir.dt.bfloat16
I32 = mybir.dt.int32
ALU = mybir.AluOpType
ACT = mybir.ActivationFunctionType
AX_X = mybir.AxisListType.X

P = 128
HEADS, HD = 16, 8
RES = 8
HG = 4
TOPK = 6
LN_EPS, FFN_EPS = 1e-5, 1e-10
SCALE = HD ** -0.5
VW = 32
SLOTS = [(0, 0), (0, 1), (0, 2), (1, 0), (1, 1), (2, 0)]
ROWS = len(SLOTS) * HD
SAFE_NORM2 = 60 * 4 / SCALE


def adaln_block(nc, x, ipw, router_w, router_b, expert_w, c, wmod, out):
    B, T, D = x.shape
    E = expert_w.shape[0]
    NT = T // P
    NG = HEADS // HG
    UNITS = HG * NT // 2
    BU = NG * UNITS
    RB = T // RES
    CE = 4
    CPT = E // CE
    CHUNKS = NT * CPT
    assert D == P and T == 512 and NT == 4 and HEADS * HD == D

    TAIL = {0: 1, 1: 2, 2: 1, 3: 2, 4: 1, 5: 2, 6: 1, 7: 1}
    HEAD = {11: 1, 12: 1, 13: 1, 14: 1, 15: 1}
    HEAD_N = sum(HEAD.values())
    assert HEAD_N + sum(TAIL.values()) == CHUNKS

    def tokens(t, b):
        return t[b].rearrange("(j r) d -> r j d", r=RES)

    keys_scr = nc.dram_tensor("keys_scr", (B, HEADS, len(SLOTS), HD, T), BF16, kind="Internal").ap()
    qry_scr = nc.dram_tensor("qry_scr", (B, 2, HEADS, 3, HD, T), BF16, kind="Internal").ap()
    guard_scr = nc.dram_tensor("guard_scr", (B, HEADS, 3, T), BF16, kind="Internal").ap()

    ctx = ExitStack()
    with ctx:
        def sb(name, shape, dt=F32):
            return ctx.enter_context(nc.sbuf_tensor(name, shape, dt))

        def sem(name):
            return ctx.enter_context(nc.semaphore(name))

        xt = sb("xt", [P, B, NT, D])
        ident = sb("ident", [P, P])
        ones = sb("ones", [P, P])
        head_sel = sb("head_sel", [P, HEADS])
        own = sb("own", [P, NT, RES])
        mask_w = sb("mask_w", [P, NT, RES])
        c_in = sb("c_in", [B, D])
        rw_in = sb("rw_in", [E, D])
        wmod_sb = sb("wmod_sb", [D, 6 * D])
        cT = sb("cT", [D, B])
        c_exp = sb("c_exp", [D, B])
        siluT = sb("siluT", [D, B])
        rwT = sb("rwT", [D, E])
        rb = sb("rb", [P, E])
        we = sb("we", [D, E, D])
        modT = sb("modT", [D, 6, B])
        gates = sb("gates", [D, 3, B])
        gate_tmp = sb("gate_tmp", [D, 2, B])
        gate_rows = sb("gate_rows", [P, 3, B, D])
        wcol = sb("wcol", [P, 4])
        bound = sb("bound", [P, 2])
        bound1 = sb("bound1", [1, 4])
        unsafe = sb("unsafe", [1, 1], I32)

        stats = sb("stats", [P, NT, 6])
        mv = sb("mv", [P, NT, 2])
        stats2 = sb("stats2", [P, NT, 6])
        mv2 = sb("mv2", [P, NT, 2])
        nr = sb("nr", [P, 5, NT])
        xs = sb("xs", [P, NT, D])
        h3 = sb("h3", [D, 3, T])
        hres = sb("hres", [D, 3, T])
        parts = sb("parts", [D, 3, 3, T], BF16)
        sq = sb("sq", [D, T])
        g_neg = sb("g_neg", [HEADS, T])
        g_res = sb("g_res", [HEADS, T])
        g_parts = sb("g_parts", [HEADS, 3, T], BF16)
        h_one = sb("h_one", [D, T])
        blk = sb("blk", [P, 2, RES])
        rowmax = sb("rowmax", [P, NT, HEADS])

        keys = sb("keys", [P, 2, HG, T], BF16)
        qry_w = sb("qry_w", [P, 2, HG, T], BF16)
        qry_c = sb("qry_c", [P, 2, HG, T], BF16)
        vals = sb("vals", [P, NT, HEADS, VW])
        probs = sb("probs", [P, 2, HG, NT, T])
        o_sb = sb("o_sb", [P, T])
        rden = sb("rden", [P, NT, HG])
        att = sb("att", [P, NT, HEADS, HD])

        xs2 = sb("xs2", [P, NT, D])
        nr2 = sb("nr2", [P, 5, NT])
        x2a = sb("x2a", [P, NT, D])
        x2b = sb("x2b", [P, NT, D])
        h2 = sb("h2", [D, T])
        lgt = sb("lgt", [P, NT, E])
        lmx = sb("lmx", [P, NT])
        pex = sb("pex", [P, NT, E])
        pz = sb("pz", [P, 6, NT])
        prb = sb("prb", [P, NT, E + 2])
        top8 = sb("top8", [P, NT, 8])
        rest = sb("rest", [P, NT, E + 2])
        gsel = sb("gsel", [P, NT, E])
        gate = sb("gate", [P, NT, E])
        gate_n = sb("gate_n", [P, NT, E])
        eps_row = sb("eps_row", [P, NT])
        acc = sb("acc", [P, NT, CE, D])
        acc2 = sb("acc2", [P, NT, 2, D])

        ps = ctx.enter_context(nc.psum_tensor("ps", [P, 8, T], F32))
        SUMS, TURN, EXPERT = 4, 5, 6

        consts_in = sem("consts_in")
        small_in = sem("small_in")
        x0_in = sem("x0_in")
        x_in = sem("x_in")
        we_in = sem("we_in")
        pool_set = sem("pool_set")
        dve_set = sem("dve_set")
        pe_set = sem("pe_set")
        act_set = sem("act_set")
        dve_chain = sem("dve_chain")
        diag_set = sem("diag_set")
        rows_done = sem("rows_done")
        flag_set = sem("flag_set")
        prep_chain = sem("prep_chain")
        res_chain = sem("res_chain")
        gate_chain = sem("gate_chain")
        fin_chain = sem("fin_chain")
        den_chain = sem("den_chain")
        nwt_chain = sem("nwt_chain")
        nwt2_chain = sem("nwt2_chain")
        seeded = sem("seeded")
        rstd_done = sem("rstd_done")
        seeded2 = sem("seeded2")
        rstd2_done = sem("rstd2_done")
        xs_done = sem("xs_done")
        vals_done = sem("vals_done")
        hT_turned = sem("hT_turned")
        hT_done = sem("hT_done")
        sq_done = sem("sq_done")
        split_done = sem("split_done")
        guard_psum = sem("guard_psum")
        guard_read = sem("guard_read")
        guard_done = sem("guard_done")
        stored = sem("stored")
        loaded = [sem("loaded0"), sem("loaded1")]
        one_done = sem("one_done")
        one_score = sem("one_score")
        one_used = sem("one_used")
        rowmax_done = sem("rowmax_done")
        scored = sem("scored")
        expd = sem("expd")
        summed = sem("summed")
        sums_out = sem("sums_out")
        sums_turned = sem("sums_turned")
        att_done = sem("att_done")
        xs2_done = sem("xs2_done")
        h2_turned = sem("h2_turned")
        h2_done = sem("h2_done")
        logits = sem("logits")
        logits_read = sem("logits_read")
        lgt_done = sem("lgt_done")
        pex_done = sem("pex_done")
        expert = sem("expert")
        expert_used = sem("expert_used")
        y_done = sem("y_done")
        y_out = sem("y_out")

        def after(eng, s, n):
            if not (isinstance(n, int) and n <= 0):
                eng.wait_ge(s, n)

        def apart(eng, s, n):
            after(eng, s, n)
            if not isinstance(n, int):
                eng.nop(nofuse=True)

        class Chain:
            def __init__(self, s, per=0):
                self.s, self.per = s, per

            def start(self, eng, n):
                self.eng, self.n, self.k = eng, n, 0

            def link(self, ins, alone=False):
                self.k += 1
                ins.then_inc(self.s, 1)
                (apart if alone else after)(self.eng, self.s, self.n * self.per + self.k)

            def end(self):
                assert self.per in (0, self.k)
                self.per = self.k

        def schedule(eng, body):
            body(0, tail=False, head=False, prep=True)
            body(1, tail=False, head=True, prep=True)
            with eng.Fori(2, B - 1) as b:
                body(b, tail=True, head=True, prep=True)
            body(B - 1, tail=True, head=True, prep=False)

        def chunk_list(table, base):
            out_, k = {}, base
            for s in range(16):
                out_[s] = list(range(k, k + table.get(s, 0)))
                k += table.get(s, 0)
            return out_
        head_chunks = chunk_list(HEAD, 0)
        tail_chunks = chunk_list(TAIL, HEAD_N)

        block = ctx.enter_context(nc.Block())

        @block.sync
        def _(sp):
            sp.dma_start(c_in[:, :], c).then_inc(small_in, 16)
            sp.dma_start(rw_in[:, :], router_w).then_inc(small_in, 16)
            sp.dma_start(wcol[:, 0:1], bass.AP(ipw.tensor, 0, [[0, P], [1, 1]])).then_inc(small_in, 16)
            for r in range(RES):
                lo = r % 2 * RB
                sp.dma_start(xt[lo:lo + RB, 0, r // 2, :], tokens(x, 0)[r]).then_inc(x0_in, 16)
            sp.dma_start(wmod_sb[:, :], wmod).then_inc(consts_in, 16)
            sp.dma_start(rb[:, :], bass.AP(router_b.tensor, 0, [[0, P], [1, E]])).then_inc(consts_in, 16)
            for b in range(1, B):
                for r in range(RES):
                    lo = r % 2 * RB
                    sp.dma_start(xt[lo:lo + RB, b, r // 2, :], tokens(x, b)[r]).then_inc(x_in, 16)
            sp.dma_start(we[:, :, :], expert_w.rearrange("e d n -> d e n")).then_inc(we_in, 16)

            def store(b):
                apart(sp, split_done, b + 1)
                for slot, (kp, _) in enumerate(SLOTS):
                    sp.dma_start(keys_scr[b, :, slot], parts[:, 0, kp, :]).then_inc(stored, 16)
                for v in range(2):
                    for part in range(3):
                        sp.dma_start(qry_scr[b, v, :, part], parts[:, 1 + v, part, :]).then_inc(stored, 16)
                apart(sp, guard_done, b + 1)
                sp.dma_start(guard_scr[b], g_parts[:, :, :]).then_inc(stored, 16)

            STORES = 16 * (len(SLOTS) + 2 * 3 + 1)

            def load(b, t):
                slot, h0 = t % 2, HG * t
                done = loaded[slot]
                k = keys_scr[b, h0:h0 + HG].rearrange("h s d n -> (s d) h n")
                sp.dma_start(keys[0:ROWS, slot, :, :], k).then_inc(done, 16)
                for v, dst in ((0, qry_w), (1, qry_c)):
                    row = 0
                    for n in (3, 2, 1):
                        q = qry_scr[b, v, h0:h0 + HG, 0:n].rearrange("h a d n -> (a d) h n")
                        sp.dma_start(dst[row:row + n * HD, slot, :, :], q).then_inc(done, 16)
                        row += n * HD
                g = guard_scr[b, h0:h0 + HG].rearrange("h a n -> a h n")
                sp.dma_start(qry_w[ROWS:ROWS + 3, slot, :, :], g).then_inc(done, 16)

            def put_out(b):
                apart(sp, y_done, b + 1)
                for r in range(RES):
                    lo = r % 2 * RB
                    sp.dma_start(tokens(out, b)[r], xt[lo:lo + RB, b, r // 2, :]).then_inc(y_out, 16)

            def body(b, tail, head, prep):
                for t in range(NG):
                    if t == 1 and prep:
                        store(b + 1)
                    apart(sp, scored, b * BU + (t + 1) * UNITS)
                    if t < 2:
                        load(b, t + 2)
                    elif prep:
                        if t == 2:
                            apart(sp, stored, (b + 2) * STORES)
                        load(b + 1, t - 2)
                    if t == 2 and tail:
                        put_out(b - 2)

            sp.wait_ge(pool_set, 12)
            store(0)
            sp.wait_ge(stored, STORES)
            load(0, 0)
            load(0, 1)
            schedule(sp, body)
            put_out(B - 2)
            put_out(B - 1)
            sp.wait_ge(y_out, 16 * RES * B)

        @block.gpsimd
        def _(pool):
            def put(ins):
                ins.then_inc(pool_set, 1)
            put(pool.memset(ident[:, :], 0.0))
            put(pool.memset(ones[:, :], 1.0))
            put(pool.memset(head_sel[:, :], 1.0))
            pool.wait_ge(pool_set, 3)
            put(pool.affine_select(out=ident[:, :], in_=ident[:, :], compare_op=ALU.not_equal, fill=1.0,
                                   base=0, pattern=[[-1, P]], channel_multiplier=1))
            put(pool.affine_select(out=head_sel[:, :], in_=head_sel[:, :], compare_op=ALU.is_ge, fill=0.0,
                                   base=0, pattern=[[-HD, HEADS]], channel_multiplier=1))
            pool.wait_ge(pool_set, 5)
            put(pool.affine_select(out=head_sel[:, :], in_=head_sel[:, :], compare_op=ALU.is_ge, fill=0.0,
                                   base=HD - 1, pattern=[[HD, HEADS]], channel_multiplier=-1))
            put(pool.memset(keys[:, :, :, :], 0.0))
            pool.wait_ge(pool_set, 7)
            put(pool.memset(keys[32:64, :, :, :], 1.0))
            pool.wait_ge(pool_set, 8)
            put(pool.memset(qry_w[:, :, :, :], 0.0))
            put(pool.memset(qry_c[:, :, :, :], 0.0))
            put(pool.memset(vals[:, :, :, :], 0.0))
            pool.wait_ge(pool_set, 11)
            put(pool.memset(vals[:, :, :, HD:HD + 1], 1.0))

            def newton(chain, n, nrt, seeded_s, done):
                pool.wait_ge(seeded_s, n + 1)
                chain.start(pool, n)
                y, u = nrt[:, 2, :], nrt[:, 3, :]
                for k in range(3):
                    chain.link(pool.tensor_tensor(u, y, y, ALU.mult))
                    chain.link(pool.tensor_tensor(u, u, nrt[:, 1, :], ALU.mult), alone=True)
                    chain.link(pool.tensor_scalar(u, u, 1.5, None, ALU.add))
                    ins = pool.tensor_tensor(y, y, u, ALU.mult)
                    if k < 2:
                        chain.link(ins)
                ins.then_inc(done, 1)
                chain.end()

            nwt, nwt2 = Chain(nwt_chain), Chain(nwt2_chain)

            def prep_a(n):
                newton(nwt, n, nr, seeded, rstd_done)

            def prep_b(n):
                pool.wait_ge(hT_done, n + 1)
                after(pool, guard_psum, n)
                pool.tensor_tensor(sq[:, :], h3[:, 0, :], h3[:, 0, :], ALU.mult).then_inc(sq_done, 1)

            def put_vals(b, t):
                apart(pool, xs_done, b + 1)
                apart(pool, summed, (b - 1) * NG + t + 1)
                src = xs[:, :, :].rearrange("p i (h d) -> p i h d", d=HD)[:, :, HG * t:HG * t + HG, :]
                pool.tensor_copy(vals[:, :, HG * t:HG * t + HG, 0:HD], src).then_inc(vals_done, 1)

            def body(b, tail, head, prep):
                if prep:
                    prep_a(b + 1)
                put_vals(b, NG - 1)
                if prep:
                    prep_b(b + 1)
                if head:
                    newton(nwt2, b - 1, nr2, seeded2, rstd2_done)
                if prep:
                    for t in range(NG - 1):
                        put_vals(b + 1, t)

            prep_a(0)
            for t in range(NG - 1):
                put_vals(0, t)
            prep_b(0)
            schedule(pool, body)
            newton(nwt2, B - 1, nr2, seeded2, rstd2_done)

        @block.scalar
        def _(act):
            act.wait_ge(small_in, 48)
            act.activation(wcol[:, 1:2], wcol[:, 0:1], ACT.Exp, scale=-1.0).then_inc(act_set, 1)
            act.wait_ge(dve_set, 1)
            act.activation(c_exp[:, :], cT[:, :], ACT.Exp, scale=-1.0).then_inc(act_set, 1)

            def h_out(n):
                act.wait_ge(hT_turned, n + 1)
                after(act, split_done, n)
                after(act, sq_done, n)
                after(act, guard_psum, n)
                act.activation(h3[:, 0, :], ps[:, TURN, :], ACT.Identity, bias=modT[:, 0, bass.ds(n, 1)],
                               scale=modT[:, 1, bass.ds(n, 1)]).then_inc(hT_done, 1)

            def h2_out(n):
                act.wait_ge(h2_turned, n + 1)
                after(act, expert, n * CHUNKS)
                act.activation(h2[:, :], ps[:, TURN, :], ACT.Identity, bias=modT[:, 3, bass.ds(n, 1)],
                               scale=modT[:, 4, bass.ds(n, 1)]).then_inc(h2_done, 1)

            def router_exp(n):
                act.wait_ge(lgt_done, n + 1)
                act.activation(pex[:, :, :], lgt[:, :, :], ACT.Exp).then_inc(pex_done, 1)

            def sums_copy(g):
                act.wait_ge(summed, g + 1)
                after(act, sums_turned, g)
                act.activation(o_sb[:, :], ps[:, SUMS, :], ACT.Copy).then_inc(sums_out, 1)

            def exps(b, t, hh):
                if hh == 0:
                    after(act, summed, b * NG + t - 1)
                for p in range(2):
                    u = t * UNITS + 2 * hh + p
                    act.wait_ge(scored, b * BU + u + 1)
                    bank = 2 * p
                    act.activation(probs[:, t % 2, hh, 2 * p:2 * p + 2, :], ps[:, bank:bank + 2, :],
                                   ACT.Exp, scale=SCALE).then_inc(expd, 1)

            def body(b, tail, head, prep):
                for s in range(16):
                    t, hh = divmod(s, HG)
                    first = isinstance(b, int) and b * NG + t < 2
                    if hh == 0 and not first:
                        sums_copy(b * NG + t - 2)
                    exps(b, t, hh)
                    if s == 4 and prep:
                        h_out(b + 1)
                    if s == 8 and head:
                        h2_out(b - 1)
                    if s == 10 and head:
                        router_exp(b - 1)

            act.wait_ge(dve_set, 4)
            h_out(0)
            for k in range(3):
                for half in range(2):
                    n = 2 * k + half
                    act.wait_ge(rows_done, n + 1)
                    src = ps[:, EXPERT + n % 2, :].rearrange("p (b d) -> p b d", d=D)
                    act.activation(gate_rows[:, k, 4 * half:4 * half + 4, :], src, ACT.Copy).then_inc(act_set, 1)
            schedule(act, body)
            sums_copy(B * NG - 2)
            sums_copy(B * NG - 1)
            h2_out(B - 1)
            router_exp(B - 1)

        @block.vector
        def _(dve):
            n_setup = [0]

            def link(ins):
                n_setup[0] += 1
                ins.then_inc(dve_chain, 1)
                dve.wait_ge(dve_chain, n_setup[0])

            prep_c, res_c, gate_c, fin_c = Chain(prep_chain), Chain(res_chain), Chain(gate_chain), Chain(fin_chain, per=3)

            def moments(chain, src, stats, mv, nrt, seeded_s):
                for i in range(NT):
                    ins = dve.bn_stats(stats[:, i, :], src[:, i, :])
                chain.link(ins, alone=True)
                for i in range(NT):
                    ins = dve.bn_aggr(mv[:, i, :], stats[:, i, :])
                chain.link(ins)
                chain.link(dve.tensor_scalar(nrt[:, 0, :], mv[:, :, 1], LN_EPS, None, ALU.add))
                dve.tensor_scalar(nrt[:, 1, :], nrt[:, 0, :], -0.5, None, ALU.mult)
                chain.link(dve.tensor_scalar(nrt[:, 4, :].bitcast(I32), nrt[:, 0, :].bitcast(I32), 1, None,
                                             ALU.arith_shift_right))
                dve.tensor_scalar(nrt[:, 2, :].bitcast(I32), nrt[:, 4, :].bitcast(I32), -1.0,
                                  float(0x5F3759DF), ALU.mult, ALU.add).then_inc(seeded_s, 1)

            def normalise(dst, src, mv, nrt, done):
                for i in range(NT):
                    ins = dve.tensor_scalar(dst[:, i, :], src[:, i, :], mv[:, i, 0:1], nrt[:, 2, i:i + 1],
                                            ALU.subtract, ALU.mult)
                ins.then_inc(done, 1)

            def prep_ln(n):
                prep_c.start(dve, n)
                moments(prep_c, xt[:, n], stats, mv, nr, seeded)

            def prep_xs(n):
                dve.wait_ge(rstd_done, n + 1)
                after(dve, vals_done, n * NG)
                after(dve, hT_turned, n)
                normalise(xs, xt[:, n], mv, nr, xs_done)

            def prep_split(n):
                dve.wait_ge(hT_done, n + 1)
                after(dve, stored, n * 16 * (len(SLOTS) + 2 * 3 + 1))
                dve.tensor_scalar(h3[:, 1, :], h3[:, 0, :], wcol[:, 2:3], None, ALU.mult)
                prep_c.link(dve.tensor_scalar(h3[:, 2, :], h3[:, 0, :], wcol[:, 3:4], None, ALU.mult))
                prep_c.link(dve.tensor_copy(parts[:, :, 0, :], h3[:, :, :]))
                prep_c.link(dve.tensor_tensor(hres[:, :, :], h3[:, :, :], parts[:, :, 0, :], ALU.subtract))
                prep_c.link(dve.tensor_copy(parts[:, :, 1, :], hres[:, :, :]))
                dve.tensor_tensor(parts[:, :, 2, :], hres[:, :, :], parts[:, :, 1, :],
                                  ALU.subtract).then_inc(split_done, 1)

            def true_max(n):
                with dve.Fori(0, HEADS) as h:
                    dve.tensor_scalar(h_one[:, :], h3[:, 0, :], head_sel[:, bass.ds(h, 1)], None,
                                      ALU.mult).then_inc(one_done, 1)
                    for i in range(NT):
                        k = n * HEADS * NT + h * NT + i
                        dve.wait_ge(one_score, k + 1)
                        src = ps[:, EXPERT + 1, :].rearrange("p (r j) -> p r j", r=RES)
                        dve.tensor_reduce(blk[:, 0, :], src, AX_X, ALU.max).then_inc(one_used, 1)
                        dve.wait_ge(one_used, 3 * k + 1)
                        dve.tensor_tensor(blk[:, 1, :], blk[:, 0, :], mask_w[:, i, :],
                                          ALU.mult).then_inc(one_used, 1)
                        dve.wait_ge(one_used, 3 * k + 2)
                        dve.tensor_reduce(rowmax[:, i, bass.ds(h, 1)], blk[:, 1, :], AX_X,
                                          ALU.max).then_inc(one_used, 1)
                        dve.wait_ge(one_used, 3 * k + 3)
                dve.engine_nop().then_inc(rowmax_done, 1)

            def prep_guard(n):
                prep_c.eng = dve
                dve.wait_ge(guard_psum, n + 1)
                prep_g = ps[0:HEADS, TURN, :]
                ins = dve.tensor_scalar(g_neg[:, :], prep_g, -1.0, None, ALU.mult)
                ins.then_inc(guard_read, 1)
                dve.wait_ge(guard_read, n + 1)
                prep_c.link(dve.tensor_copy(g_parts[:, 0, :], g_neg[:, :]))
                prep_c.link(dve.tensor_tensor(g_res[:, :], g_neg[:, :], g_parts[:, 0, :], ALU.subtract))
                prep_c.link(dve.tensor_copy(g_parts[:, 1, :], g_res[:, :]))
                dve.tensor_tensor(g_parts[:, 2, :], g_res[:, :], g_parts[:, 1, :],
                                  ALU.subtract).then_inc(guard_done, 1)
                prep_c.end()

            def finish_group(g, t):
                dve.wait_ge(sums_turned, g + 1)
                src = ps[:, TURN, :].rearrange("p (i h v) -> p i h v", i=NT, v=VW)
                dve.reciprocal(rden[:, :, :], src[:, :, :, HD]).then_inc(den_chain, 1)
                dve.wait_ge(den_chain, g + 1)
                dve.tensor_tensor(att[:, :, HG * t:HG * t + HG, :], src[:, :, :, 0:HD],
                                  rden[:, :, :].unsqueeze(3).to_broadcast([P, NT, HG, HD]),
                                  ALU.mult).then_inc(att_done, 1)

            def rows(k, n):
                return gate_rows[:, k, bass.ds(n, 1), :].to_broadcast([P, NT, D])

            def residual(n):
                dve.wait_ge(att_done, (n + 1) * NG)
                res_c.start(dve, n)
                res_c.link(dve.tensor_tensor(x2a[:, :, :], att[:, :, :, :].rearrange("p i h d -> p i (h d)"),
                                             rows(0, n), ALU.mult))
                res_c.link(dve.tensor_tensor(x2b[:, :, :], x2a[:, :, :], rows(1, n), ALU.add))
                res_c.link(dve.tensor_tensor(xt[:, n], xt[:, n], x2b[:, :, :], ALU.add), alone=True)
                moments(res_c, xt[:, n], stats2, mv2, nr2, seeded2)

            def second_ln(n):
                dve.wait_ge(rstd2_done, n + 1)
                after(dve, h2_turned, n)
                normalise(xs2, xt[:, n], mv2, nr2, xs2_done)
                res_c.end()

            def wide(t_, n_=E):
                return t_.unsqueeze(2).to_broadcast([P, NT, n_])

            def router(n):
                dve.wait_ge(logits, n + 1)
                gate_c.start(dve, n)
                lp = ps[:, TURN, 0:NT * E].rearrange("p (i e) -> p i e", e=E)
                dve.tensor_tensor(lgt[:, :, :], lp, rb[:, :].unsqueeze(1).to_broadcast([P, NT, E]),
                                  ALU.add).then_inc(logits_read, 1)
                dve.wait_ge(logits_read, n + 1)
                gate_c.link(dve.tensor_reduce(lmx[:, :], lgt[:, :, :], AX_X, ALU.max))
                dve.tensor_tensor(lgt[:, :, :], lgt[:, :, :], wide(lmx[:, :]), ALU.subtract).then_inc(lgt_done, 1)

            def router_gates(n):
                dve.wait_ge(pex_done, n + 1)
                gate_c.link(dve.tensor_reduce(pz[:, 0, :], pex[:, :, :], AX_X, ALU.add))
                gate_c.link(dve.reciprocal(pz[:, 1, :], pz[:, 0, :]))
                gate_c.link(dve.tensor_tensor(prb[:, :, 0:E], pex[:, :, :], wide(pz[:, 1, :]), ALU.mult), alone=True)
                for i in range(NT):
                    ins = dve.max(top8[:, i, :], prb[:, i, 0:E])
                gate_c.link(ins)
                gate_c.link(dve.tensor_copy(top8[:, :, TOPK:8], prb[:, :, E:E + 2]), alone=True)
                for i in range(NT):
                    ins = dve.match_replace(rest[:, i, :], top8[:, i, :], prb[:, i, :], 0.0)
                gate_c.link(ins)
                gate_c.link(dve.tensor_tensor(gsel[:, :, :], prb[:, :, 0:E], rest[:, :, 0:E], ALU.subtract))
                gate_c.link(dve.tensor_reduce(pz[:, 2, :], gsel[:, :, :], AX_X, ALU.add))
                gate_c.link(dve.tensor_scalar(pz[:, 2, :], pz[:, 2, :], FFN_EPS, None, ALU.add))
                gate_c.link(dve.reciprocal(pz[:, 3, :], pz[:, 2, :]))
                gate_c.link(dve.tensor_tensor(gate[:, :, :], gsel[:, :, :], wide(pz[:, 3, :]), ALU.mult))
                gate_c.link(dve.tensor_reduce(pz[:, 4, :], gate[:, :, :], AX_X, ALU.add))
                dve.tensor_scalar(eps_row[:, :], pz[:, 4, :], FFN_EPS, None, ALU.mult)
                gate_c.link(dve.tensor_scalar(pz[:, 5, :], pz[:, 4, :], FFN_EPS, None, ALU.max))
                gate_c.link(dve.reciprocal(pz[:, 0, :], pz[:, 5, :]))
                gate_c.link(dve.tensor_tensor(gate_n[:, :, :], gate[:, :, :], wide(pz[:, 0, :]), ALU.mult))
                gate_c.end()

            def experts(n, q):
                i, cc = divmod(q, CPT)
                dve.wait_ge(expert, n * CHUNKS + q + 1)
                after(dve, expert_used, n * CHUNKS + q)
                for k in range(CE):
                    e = CE * cc + k
                    src = ps[:, EXPERT + q % 2, k * D:(k + 1) * D]
                    g = gate_n[:, i, e:e + 1]
                    if cc:
                        ins = dve.scalar_tensor_tensor(acc[:, i, k, :], src, g, acc[:, i, k, :], ALU.mult, ALU.add)
                    elif k == 0:
                        ins = dve.tensor_scalar(acc[:, i, k, :], src, g, eps_row[:, i:i + 1], ALU.mult, ALU.add)
                    else:
                        ins = dve.tensor_scalar(acc[:, i, k, :], src, g, None, ALU.mult)
                ins.then_inc(expert_used, 1)

            def finish(n):
                dve.wait_ge(expert_used, (n + 1) * CHUNKS)
                fin_c.start(dve, n)
                fin_c.link(dve.tensor_tensor(acc2[:, :, :, :], acc[:, :, 0:2, :], acc[:, :, 2:4, :], ALU.add))
                fin_c.link(dve.tensor_tensor(x2a[:, :, :], acc2[:, :, 0, :], acc2[:, :, 1, :], ALU.add))
                fin_c.link(dve.tensor_tensor(x2b[:, :, :], x2a[:, :, :], rows(2, n), ALU.mult))
                dve.tensor_tensor(xt[:, n], xt[:, n], x2b[:, :, :], ALU.add).then_inc(y_done, 1)
                dve.wait_ge(y_done, n + 1)
                fin_c.end()

            dve.memset(own[:, :, :], 0.0).then_inc(dve_chain, 1)
            dve.memset(prb[:, :, E:E + 1], -1.0).then_inc(dve_chain, 1)
            dve.memset(prb[:, :, E + 1:E + 2], -2.0).then_inc(dve_chain, 1)
            n_setup[0] = 3
            dve.wait_ge(dve_chain, 3)
            for i in range(NT):
                dve.memset(own[0:RB, i, 2 * i:2 * i + 1], 1.0)
                ins = dve.memset(own[RB:P, i, 2 * i + 1:2 * i + 2], 1.0)
            link(ins)
            dve.wait_ge(pe_set, 1)
            dve.tensor_copy(cT[:, :], ps[:, TURN, 0:B]).then_inc(dve_set, 1)
            link(dve.tensor_copy(rwT[:, :], ps[:, TURN, B:B + E]))
            dve.wait_ge(x0_in, 16 * RES)
            dve.wait_ge(act_set, 2)
            link(dve.tensor_scalar(c_exp[:, :], c_exp[:, :], 1.0, None, ALU.add))
            link(dve.reciprocal(c_exp[:, :], c_exp[:, :]))
            dve.tensor_tensor(siluT[:, :], cT[:, :], c_exp[:, :], ALU.mult).then_inc(dve_set, 1)
            link(dve.tensor_scalar(wcol[:, 1:2], wcol[:, 1:2], 1.0, None, ALU.add))
            link(dve.reciprocal(wcol[:, 2:3], wcol[:, 1:2]))
            link(dve.tensor_scalar(wcol[:, 3:4], wcol[:, 2:3], -1.0, 1.0, ALU.mult, ALU.add))
            dve.tensor_scalar(mask_w[:, :, :], own[:, :, :], wcol[:, 3:4], wcol[:, 2:3], ALU.mult,
                              ALU.add).then_inc(dve_set, 1)
            prep_ln(0)
            prep_xs(0)
            dve.wait_ge(pe_set, 2)
            link(dve.tensor_copy(modT[:, :, :], ps[:, EXPERT, 0:6 * B].rearrange("p (k b) -> p k b", b=B)))
            link(dve.tensor_scalar(modT[:, 1, :], modT[:, 1, :], 1.0, None, ALU.add))
            dve.tensor_scalar(modT[:, 4, :], modT[:, 4, :], 1.0, None, ALU.add).then_inc(dve_set, 1)
            dve.wait_ge(dve_set, 4)
            dve.tensor_reduce(bound[:, 0:1], modT[:, 1, :], AX_X, ALU.max, apply_absolute_value=True)
            dve.tensor_reduce(bound[:, 1:2], modT[:, 0, :], AX_X, ALU.max,
                              apply_absolute_value=True).then_inc(dve_set, 1)
            for k, col in ((0, 2), (1, 5)):
                dst = gates[:, 2 * k, :]
                link(dve.tensor_scalar(gate_tmp[:, 0, :], modT[:, col, :], 0.0, 2.0, ALU.is_ge, ALU.mult))
                link(dve.tensor_scalar(gate_tmp[:, 1, :], modT[:, col, :], -1.0, None, ALU.mult))
                link(dve.tensor_tensor(gate_tmp[:, 1, :], gate_tmp[:, 1, :], modT[:, col, :], ALU.max))
                link(dve.tensor_scalar(gate_tmp[:, 1, :], gate_tmp[:, 1, :], 0.25, None, ALU.max))
                link(dve.scalar_tensor_tensor(dst, gate_tmp[:, 0, :], -1.0, gate_tmp[:, 1, :], ALU.add, ALU.mult))
            link(dve.tensor_tensor(gates[:, 1, :], gates[:, 0, :], modT[:, 0, :], ALU.mult))
            link(dve.tensor_tensor(gates[:, 0, :], gates[:, 0, :], modT[:, 1, :], ALU.mult))
            dve.wait_ge(pe_set, 3)
            link(dve.tensor_reduce(bound1[:, 0:2], ps[0:1, EXPERT + 1, 0:2 * P].rearrange("p (k n) -> p k n", k=2),
                                   AX_X, ALU.max))
            link(dve.tensor_scalar(bound1[:, 2:3], bound1[:, 0:1], float(D) ** 0.5, None, ALU.mult))
            link(dve.scalar_tensor_tensor(bound1[:, 3:4], bound1[:, 1:2], float(HD) ** 0.5, bound1[:, 2:3],
                                          ALU.mult, ALU.add))
            dve.tensor_scalar(unsafe[:, :], bound1[:, 3:4], bound1[:, 3:4], float(SAFE_NORM2), ALU.mult,
                              ALU.is_gt).then_inc(flag_set, 1)
            dve.wait_ge(flag_set, 1)
            unsafe_v = dve.value_load(unsafe[0:1, 0:1], min_val=0, max_val=1)

            def guard(n):
                with dve.If(unsafe_v):
                    true_max(n)
                prep_guard(n)

            prep_split(0)
            guard(0)
            for k in range(3):
                for half in range(2):
                    n = 2 * k + half
                    after(dve, rows_done, n - 1)
                    dst = acc[:, n % 2, :, :]
                    dve.tensor_tensor(dst, ident[:, :].unsqueeze(1).to_broadcast([P, 4, P]),
                                      gates[:, k, 4 * half:4 * half + 4].unsqueeze(2).to_broadcast([P, 4, P]),
                                      ALU.mult).then_inc(diag_set, 1)
            dve.wait_ge(x_in, 16 * RES * (B - 1))
            dve.wait_ge(act_set, 8)
            dve.wait_ge(rows_done, 6)

            def body(b, tail, head, prep):
                for s in range(16):
                    t, hh = divmod(s, HG)
                    first = isinstance(b, int) and b * NG + t < 2
                    if s == 0 and prep:
                        prep_ln(b + 1)
                    if hh == 1 and not first:
                        finish_group(b * NG + t - 2, (t - 2) % NG)
                    if s == 4 and prep:
                        prep_xs(b + 1)
                    if s == 5 and head:
                        residual(b - 1)
                    if s == 6 and prep:
                        prep_split(b + 1)
                    if s == 7 and head:
                        second_ln(b - 1)
                    if s == 7 and prep:
                        guard(b + 1)
                    if s == 10 and head:
                        router(b - 1)
                        router_gates(b - 1)
                    if tail:
                        for q in tail_chunks[s]:
                            experts(b - 2, q)
                        if s == 7:
                            finish(b - 2)
                    if head:
                        for q in head_chunks[s]:
                            experts(b - 1, q)

            schedule(dve, body)
            for q in range(HEAD_N, CHUNKS):
                experts(B - 2, q)
            finish(B - 2)
            finish_group(B * NG - 2, NG - 2)
            finish_group(B * NG - 1, NG - 1)
            residual(B - 1)
            second_ln(B - 1)
            router(B - 1)
            router_gates(B - 1)
            for q in range(CHUNKS):
                experts(B - 1, q)
            finish(B - 1)

        @block.tensor
        def _(pe):
            mm = pe.matmul

            def turn4(src, done):
                for i in range(NT):
                    ins = pe.transpose(ps[:, TURN, i * P:(i + 1) * P], src(i), ident[:, :])
                ins.then_inc(done, 1)

            def prep_turn(n):
                pe.wait_ge(xs_done, n + 1)
                turn4(lambda i: xs[:, i, :], hT_turned)

            def prep_guard(n):
                with pe.If(unsafe_v):
                    with pe.Fori(0, HEADS) as h:
                        pe.wait_ge(one_done, n * HEADS + h + 1)
                        for i in range(NT):
                            k = n * HEADS * NT + h * NT + i
                            if i:
                                pe.wait_ge(one_used, 3 * k)
                            mm(ps[:, EXPERT + 1, :], h_one[:, i * P:(i + 1) * P], h3[:, 0, :], start=True,
                               stop=True).then_inc(one_score, 1)
                    pe.wait_ge(rowmax_done, n + 1)
                    for i in range(NT):
                        ins = pe.transpose(ps[0:HEADS, TURN, i * P:(i + 1) * P], rowmax[:, i, :], ident[:, :])
                    ins.then_inc(guard_psum, 1)
                with pe.Else():
                    pe.wait_ge(sq_done, n + 1)
                    mm(ps[0:HEADS, TURN, :], head_sel[:, :], sq[:, :], start=True,
                       stop=True).then_inc(guard_psum, 1)

            def scores(b, t, hh):
                if hh == 0:
                    pe.wait_ge(loaded[t % 2], (b * 2 + t // 2 + 1) * 8 * 16)
                for p in range(2):
                    u = t * UNITS + 2 * hh + p
                    after(pe, expd, b * BU + u - 1)
                    for i in (2 * p, 2 * p + 1):
                        lo, sl = i * P, t % 2
                        mm(ps[:, i, :], keys[:, sl, hh, lo:lo + P], qry_w[:, sl, hh, :], start=True, stop=False,
                           skip_group_check=True)
                        for r in range(2):
                            at = lo + r * RB
                            ins = mm(ps[r * RB:(r + 1) * RB, i, at:at + RB], keys[:, sl, hh, at:at + RB],
                                     qry_c[:, sl, hh, at:at + RB], start=False, stop=True, skip_group_check=True)
                    ins.then_inc(scored, 1)

            def sums(g, t, i):
                if i == 0:
                    pe.wait_ge(vals_done, g + 1)
                    pe.wait_ge(expd, (g + 1) * UNITS)
                    after(pe, sums_out, g)
                for hh in range(HG):
                    ins = mm(ps[VW * hh:VW * hh + VW, SUMS, :], vals[:, i, HG * t + hh, :],
                             probs[:, t % 2, hh, i, :], start=(i == 0), stop=(i == NT - 1), skip_group_check=True)
                if i == NT - 1:
                    ins.then_inc(summed, 1)

            def sums_turn(g):
                pe.wait_ge(sums_out, g + 1)
                turn4(lambda i: o_sb[:, i * P:(i + 1) * P], sums_turned)

            def h2_turn(n):
                pe.wait_ge(xs2_done, n + 1)
                turn4(lambda i: xs2[:, i, :], h2_turned)

            def route(n):
                pe.wait_ge(h2_done, n + 1)
                for i in range(NT):
                    ins = mm(ps[:, TURN, i * E:(i + 1) * E], h2[:, i * P:(i + 1) * P], rwT[:, :], start=True, stop=True)
                ins.then_inc(logits, 1)

            def experts(n, q):
                i, cc = divmod(q, CPT)
                after(pe, expert_used, n * CHUNKS + q - 1)
                mm(ps[:, EXPERT + q % 2, :], h2[:, i * P:(i + 1) * P], we[:, CE * cc:CE * cc + CE, :], start=True,
                   stop=True).then_inc(expert, 1)

            pe.wait_ge(pool_set, 4)
            pe.wait_ge(small_in, 48)
            pe.transpose(ps[:, TURN, 0:B], c_in[:, :], ident[0:B, 0:B])
            pe.transpose(ps[:, TURN, B:B + E], rw_in[:, :], ident[0:E, 0:E]).then_inc(pe_set, 1)
            pe.wait_ge(consts_in, 32)
            pe.wait_ge(dve_set, 2)
            for k in range(6):
                ins = mm(ps[:, EXPERT, k * B:(k + 1) * B], wmod_sb[:, k * D:(k + 1) * D], siluT[:, :],
                         start=True, stop=True)
            ins.then_inc(pe_set, 1)
            prep_turn(0)
            pe.wait_ge(dve_set, 5)
            for k in range(2):
                ins = pe.transpose(ps[0:1, EXPERT + 1, k * P:(k + 1) * P], bound[:, k:k + 1], ident[:, :])
            ins.then_inc(pe_set, 1)
            pe.wait_ge(flag_set, 1)
            unsafe_v = pe.value_load(unsafe[0:1, 0:1], min_val=0, max_val=1)
            pe.wait_ge(hT_done, 1)
            pe.wait_ge(pool_set, 6)
            prep_guard(0)
            for n in range(6):
                pe.wait_ge(diag_set, n + 1)
                after(pe, act_set, 2 + n - 1)
                mm(ps[:, EXPERT + n % 2, :], ones[:, :], acc[:, n % 2, :, :], start=True,
                   stop=True).then_inc(rows_done, 1)
            pe.wait_ge(act_set, 8)
            pe.wait_ge(pool_set, 12)
            pe.wait_ge(we_in, 16)

            def body(b, tail, head, prep):
                for s in range(16):
                    t, hh = divmod(s, HG)
                    g = b * NG + t
                    scores(b, t, hh)
                    if not (isinstance(b, int) and g < 1):
                        sums(g - 1, (t - 1) % NG, hh)
                    if hh == 1 and not (isinstance(b, int) and g < 2):
                        if t == 0:
                            after(pe, att_done, g - 2)
                        elif t == 1:
                            after(pe, hT_done, b + 2) if prep else after(pe, att_done, g - 2)
                        elif t == 2:
                            if head:
                                pe.wait_ge(h2_done, b)
                            elif prep:
                                pe.wait_ge(guard_read, b + 2)
                        elif t == 3:
                            if head:
                                pe.wait_ge(logits_read, b)
                            else:
                                pe.wait_ge(att_done, g - 2)
                        sums_turn(g - 2)
                    if s == 4 and prep:
                        after(pe, att_done, b * NG - 1)
                        prep_turn(b + 1)
                    if s == 7 and prep:
                        after(pe, att_done, b * NG)
                        pe.wait_ge(hT_done, b + 2)
                        prep_guard(b + 1)
                    if s == 8 and head:
                        pe.wait_ge(guard_read, b + 2) if prep else pe.wait_ge(att_done, b * NG)
                        h2_turn(b - 1)
                    if s == 10 and head:
                        pe.wait_ge(att_done, b * NG + 1)
                        route(b - 1)
                    if tail:
                        for q in tail_chunks[s]:
                            experts(b - 2, q)
                    if head:
                        for q in head_chunks[s]:
                            experts(b - 1, q)

            schedule(pe, body)
            last = B * NG - 1
            for i in range(NT):
                sums(last, NG - 1, i)
            for q in range(HEAD_N, CHUNKS):
                experts(B - 2, q)
            pe.wait_ge(att_done, last - 1)
            sums_turn(last - 1)
            pe.wait_ge(att_done, last)
            sums_turn(last)
            pe.wait_ge(att_done, last + 1)
            h2_turn(B - 1)
            pe.wait_ge(h2_done, B)
            route(B - 1)
            for q in range(CHUNKS):
                experts(B - 1, q)


_INS = ["L0_attn_x", "L0_attn_inter_palace_weight", "L0_ffn_router_w", "L0_ffn_router_b", "L0_ffn_expert_w",
        "L0_c", "L0_wmod"]


def kernel(**inputs):
    import concourse.bacc as _bacc
    from concourse.bass_utils import run_bass_kernel_spmd as _run

    nc = _bacc.Bacc("TRN2", target_bir_lowering=False, num_devices=1)
    arrays, args = {}, []
    for name in _INS:
        a = np.ascontiguousarray(inputs[name])
        a = a.reshape(a.shape or (1,))
        arrays[f"in_{name}_dram"] = a
        args.append(nc.dram_tensor(f"in_{name}_dram", a.shape, mybir.dt.from_np(a.dtype), kind="ExternalInput").ap())
    shape = inputs["L0_attn_x"].shape
    out = nc.dram_tensor("out_0_dram", shape, F32, kind="ExternalOutput").ap()
    adaln_block(nc, *args, out)
    r = _run(nc, [arrays], core_ids=[0])
    return r.results[0]["out_0_dram"]
```

```python
from contextlib import ExitStack

import numpy as np
import concourse.bass as bass
from concourse import mybir

F32 = mybir.dt.float32
BF16 = mybir.dt.bfloat16
I32 = mybir.dt.int32
ALU = mybir.AluOpType
ACT = mybir.ActivationFunctionType
AX_X = mybir.AxisListType.X

P = 128
HEADS, HD = 16, 8
RES = 8
HG = 4
TOPK = 6
LN_EPS, FFN_EPS = 1e-5, 1e-10
SCALE = HD ** -0.5
VW = 32
SLOTS = [(0, 0), (0, 1), (0, 2), (1, 0), (1, 1), (2, 0)]
ROWS = len(SLOTS) * HD
SAFE_NORM2 = 60 * 4 / SCALE


def adaln_block(nc, x, ipw, router_w, router_b, expert_w, c, wmod, out):
    B, T, D = x.shape
    E = expert_w.shape[0]
    NT = T // P
    NG = HEADS // HG
    UNITS = HG * NT // 2
    BU = NG * UNITS
    RB = T // RES
    CE = 4
    CPT = E // CE
    CHUNKS = NT * CPT
    assert D == P and T == 512 and NT == 4 and HEADS * HD == D

    TAIL = {0: 2, 1: 1, 2: 2, 3: 2, 4: 1, 5: 1, 6: 1, 7: 1, 8: 1}
    HEAD = {13: 1, 14: 1, 15: 2}
    HEAD_N = sum(HEAD.values())
    assert HEAD_N + sum(TAIL.values()) == CHUNKS

    def tokens(t, b, half):
        return t[b].rearrange("(j i two) d -> two j i d", i=NT, two=2)[half]

    keys_scr = nc.dram_tensor("keys_scr", (B, HEADS, len(SLOTS), HD, T), BF16, kind="Internal").ap()
    qry_scr = nc.dram_tensor("qry_scr", (B, 2, HEADS, 3, HD, T), BF16, kind="Internal").ap()
    guard_scr = nc.dram_tensor("guard_scr", (B, HEADS, 3, T), BF16, kind="Internal").ap()

    ctx = ExitStack()
    with ctx:
        def sb(name, shape, dt=F32):
            return ctx.enter_context(nc.sbuf_tensor(name, shape, dt))

        def sem(name):
            return ctx.enter_context(nc.semaphore(name))

        xt = sb("xt", [P, B, NT, D])
        ident = sb("ident", [P, P])
        ones = sb("ones", [P, P])
        head_sel = sb("head_sel", [P, HEADS])
        own = sb("own", [P, NT, RES])
        mask_w = sb("mask_w", [P, NT, RES])
        c_in = sb("c_in", [B, D])
        rw_in = sb("rw_in", [E, D])
        wmod_sb = sb("wmod_sb", [D, 6 * D])
        cT = sb("cT", [D, B])
        c_exp = sb("c_exp", [D, B])
        siluT = sb("siluT", [D, B])
        rwT = sb("rwT", [D, E])
        rb = sb("rb", [P, E])
        we = sb("we", [D, E, D])
        modT = sb("modT", [D, 6, B])
        gates = sb("gates", [D, 3, B])
        gate_tmp = sb("gate_tmp", [D, 2, B])
        gate_rows = sb("gate_rows", [P, 3, B, D])
        wcol = sb("wcol", [P, 4])
        bound = sb("bound", [P, 2])
        bound1 = sb("bound1", [1, 4])
        unsafe = sb("unsafe", [1, 1], I32)

        stats = sb("stats", [P, NT, 6])
        mv = sb("mv", [P, NT, 2])
        stats2 = sb("stats2", [P, NT, 6])
        mv2 = sb("mv2", [P, NT, 2])
        nr = sb("nr", [P, 5, NT])
        xs = sb("xs", [P, NT, D])
        h3 = sb("h3", [D, 3, T])
        hres = sb("hres", [D, 3, T])
        parts = sb("parts", [D, 3, 3, T], BF16)
        sq = sb("sq", [D, T])
        g_neg = sb("g_neg", [HEADS, T])
        g_res = sb("g_res", [HEADS, T])
        g_parts = sb("g_parts", [HEADS, 3, T], BF16)
        h_one = sb("h_one", [D, T])
        blk = sb("blk", [P, 2, RES])
        rowmax = sb("rowmax", [P, NT, HEADS])

        keys = sb("keys", [P, 2, HG, T], BF16)
        qry_w = sb("qry_w", [P, 2, HG, T], BF16)
        qry_c = sb("qry_c", [P, 2, HG, T], BF16)
        vals = sb("vals", [P, NT, HEADS, VW])
        probs = sb("probs", [P, 2, HG, NT, T])
        o_sb = sb("o_sb", [P, T])
        rden = sb("rden", [P, NT, HG])
        att = sb("att", [P, NT, HEADS, HD])

        xs2 = sb("xs2", [P, NT, D])
        nr2 = sb("nr2", [P, 5, NT])
        x2a = sb("x2a", [P, NT, D])
        x2b = sb("x2b", [P, NT, D])
        h2 = sb("h2", [D, T])
        lgt = sb("lgt", [P, NT, E])
        lmx = sb("lmx", [P, NT])
        pex = sb("pex", [P, NT, E])
        pz = sb("pz", [P, 6, NT])
        prb = sb("prb", [P, NT, E + 2])
        top8 = sb("top8", [P, NT, 8])
        rest = sb("rest", [P, NT, E + 2])
        gsel = sb("gsel", [P, NT, E])
        gate = sb("gate", [P, NT, E])
        gate_n = sb("gate_n", [P, NT, E])
        eps_row = sb("eps_row", [P, NT])
        acc = sb("acc", [P, NT, CE, D])
        gated = sb("gated", [P, 2, CE, D])
        acc2 = sb("acc2", [P, NT, 2, D])

        ps = ctx.enter_context(nc.psum_tensor("ps", [P, 8, T], F32))
        SUMS, TURN, EXPERT = 4, 5, 6

        consts_in = sem("consts_in")
        small_in = sem("small_in")
        rb_in = sem("rb_in")
        x0_in = sem("x0_in")
        x1_in = sem("x1_in")
        zeroed = sem("zeroed")
        x_in = sem("x_in")
        we_in = sem("we_in")
        pool_set = sem("pool_set")
        dve_set = sem("dve_set")
        pe_set = sem("pe_set")
        act_set = sem("act_set")
        dve_chain = sem("dve_chain")
        diag_set = sem("diag_set")
        rows_done = sem("rows_done")
        flag_set = sem("flag_set")
        prep_chain = sem("prep_chain")
        res_chain = sem("res_chain")
        gate_chain = sem("gate_chain")
        fin_chain = sem("fin_chain")
        den_chain = sem("den_chain")
        nwt_chain = sem("nwt_chain")
        nwt2_chain = sem("nwt2_chain")
        seeded = sem("seeded")
        rstd_done = sem("rstd_done")
        seeded2 = sem("seeded2")
        rstd2_done = sem("rstd2_done")
        xs_done = sem("xs_done")
        vals_done = sem("vals_done")
        hT_turned = sem("hT_turned")
        hT_done = sem("hT_done")
        sq_done = sem("sq_done")
        split_done = sem("split_done")
        guard_psum = sem("guard_psum")
        guard_read = sem("guard_read")
        guard_done = sem("guard_done")
        stored = sem("stored")
        loaded = [sem("loaded0"), sem("loaded1")]
        scaled_done = sem("scaled_done")
        hi_done = sem("hi_done")
        hres_done = sem("hres_done")
        mid_done = sem("mid_done")
        g_hi_done = sem("g_hi_done")
        g_res_done = sem("g_res_done")
        g_mid_done = sem("g_mid_done")
        added = sem("added")
        one_done = sem("one_done")
        one_score = sem("one_score")
        one_used = sem("one_used")
        rowmax_done = sem("rowmax_done")
        scored = sem("scored")
        expd = sem("expd")
        summed = sem("summed")
        sums_out = sem("sums_out")
        sums_turned = sem("sums_turned")
        att_done = sem("att_done")
        xs2_done = sem("xs2_done")
        h2_turned = sem("h2_turned")
        h2_done = sem("h2_done")
        logits = sem("logits")
        logits_read = sem("logits_read")
        lgt_done = sem("lgt_done")
        pex_done = sem("pex_done")
        expert = sem("expert")
        expert_used = sem("expert_used")
        y_done = sem("y_done")
        y_out = sem("y_out")

        def after(eng, s, n):
            if not (isinstance(n, int) and n <= 0):
                eng.wait_ge(s, n)

        def apart(eng, s, n):
            after(eng, s, n)
            if not isinstance(n, int):
                eng.nop(nofuse=True)

        class Chain:
            def __init__(self, s, per=0):
                self.s, self.per = s, per

            def start(self, eng, n):
                self.eng, self.n, self.k = eng, n, 0

            def link(self, ins, alone=False):
                self.k += 1
                ins.then_inc(self.s, 1)
                (apart if alone else after)(self.eng, self.s, self.n * self.per + self.k)

            def end(self):
                assert self.per in (0, self.k)
                self.per = self.k

        def schedule(eng, body):
            body(0, tail=False, head=False, prep=True)
            body(1, tail=False, head=True, prep=True)
            with eng.Fori(2, B - 1) as b:
                body(b, tail=True, head=True, prep=True)
            body(B - 1, tail=True, head=True, prep=False)

        def chunk_list(table, base):
            out_, k = {}, base
            for s in range(16):
                out_[s] = list(range(k, k + table.get(s, 0)))
                k += table.get(s, 0)
            return out_
        head_chunks = chunk_list(HEAD, 0)
        tail_chunks = chunk_list(TAIL, HEAD_N)

        STORES = 16 * (len(SLOTS) + 2 * 3 + 1)
        ROWS_AT = 8

        block = ctx.enter_context(nc.Block())

        @block.sync
        def _(sp):
            def load_x(b, done):
                for half in range(2):
                    sp.dma_start(xt[half * RB:half * RB + RB, b, :, :], tokens(x, b, half)).then_inc(done, 16)

            load_x(0, x0_in)
            sp.dma_start(wmod_sb[:, :], wmod).then_inc(consts_in, 16)

            def store(b):
                apart(sp, split_done, b + 1)
                for slot, (kp, _) in enumerate(SLOTS):
                    sp.dma_start(keys_scr[b, :, slot], parts[:, 0, kp, :]).then_inc(stored, 16)
                for v in range(2):
                    for part in range(3):
                        sp.dma_start(qry_scr[b, v, :, part], parts[:, 1 + v, part, :]).then_inc(stored, 16)
                apart(sp, guard_done, b + 1)
                sp.dma_start(guard_scr[b], g_parts[:, :, :]).then_inc(stored, 16)

            def load(b, t):
                slot, h0 = t % 2, HG * t
                done = loaded[slot]
                k = keys_scr[b, h0:h0 + HG].rearrange("h s d n -> (s d) h n")
                sp.dma_start(keys[0:ROWS, slot, :, :], k).then_inc(done, 16)
                for v, dst in ((0, qry_w), (1, qry_c)):
                    row = 0
                    for n in (3, 2, 1):
                        q = qry_scr[b, v, h0:h0 + HG, 0:n].rearrange("h a d n -> (a d) h n")
                        sp.dma_start(dst[row:row + n * HD, slot, :, :], q).then_inc(done, 16)
                        row += n * HD
                g = guard_scr[b, h0:h0 + HG].rearrange("h a n -> a h n")
                sp.dma_start(qry_w[ROWS:ROWS + 3, slot, :, :], g).then_inc(done, 16)

            def put_out(b):
                apart(sp, y_done, b + 1)
                for half in range(2):
                    sp.dma_start(tokens(out, b, half), xt[half * RB:half * RB + RB, b, :, :]).then_inc(y_out, 16)

            def body(b, tail, head, prep):
                for t in range(NG):
                    if t == 2 and prep:
                        store(b + 1)
                    apart(sp, scored, b * BU + (t + 1) * UNITS)
                    if t < 2:
                        load(b, t + 2)
                    elif prep:
                        if t == 2:
                            apart(sp, stored, (b + 2) * STORES)
                        load(b + 1, t - 2)
                    if t == 2 and tail:
                        put_out(b - 2)

            sp.wait_ge(pool_set, 9)
            sp.wait_ge(zeroed, 3)
            store(0)
            sp.wait_ge(stored, STORES)
            load(0, 0)
            load(0, 1)
            load_x(1, x1_in)
            sp.dma_start(rb[:, :], bass.AP(router_b.tensor, 0, [[0, P], [1, E]])).then_inc(rb_in, 16)
            sp.dma_start(we[:, :, :], expert_w.rearrange("e d n -> d e n")).then_inc(we_in, 16)
            for b in range(2, B):
                load_x(b, x_in)
            schedule(sp, body)
            put_out(B - 2)
            put_out(B - 1)
            sp.wait_ge(y_out, 16 * 2 * B)

        @block.gpsimd
        def _(pool):
            def put(ins):
                ins.then_inc(pool_set, 1)
            put(pool.memset(ident[:, :], 0.0))
            put(pool.memset(ones[:, :], 1.0))
            put(pool.memset(head_sel[:, :], 1.0))
            pool.wait_ge(pool_set, 3)
            put(pool.affine_select(out=ident[:, :], in_=ident[:, :], compare_op=ALU.not_equal, fill=1.0,
                                   base=0, pattern=[[-1, P]], channel_multiplier=1))
            put(pool.affine_select(out=head_sel[:, :], in_=head_sel[:, :], compare_op=ALU.is_ge, fill=0.0,
                                   base=0, pattern=[[-HD, HEADS]], channel_multiplier=1))
            pool.wait_ge(pool_set, 5)
            put(pool.affine_select(out=head_sel[:, :], in_=head_sel[:, :], compare_op=ALU.is_ge, fill=0.0,
                                   base=HD - 1, pattern=[[HD, HEADS]], channel_multiplier=-1))

            def stack_consts():
                put(pool.memset(keys[:, :, :, :].bitcast(F32), 0.0))
                pool.wait_ge(pool_set, 7)
                put(pool.memset(keys[32:64, :, :, :], 1.0))
                pool.wait_ge(pool_set, 8)
                pool.wait_ge(zeroed, 3)
                put(pool.memset(vals[:, :, :, HD:HD + 1], 1.0))

            def newton(chain, n, nrt, seeded_s, done):
                pool.wait_ge(seeded_s, n + 1)
                chain.start(pool, n)
                y, u = nrt[:, 2, :], nrt[:, 3, :]
                for k in range(3):
                    chain.link(pool.tensor_tensor(u, y, y, ALU.mult))
                    chain.link(pool.tensor_tensor(u, u, nrt[:, 1, :], ALU.mult), alone=True)
                    chain.link(pool.tensor_scalar(u, u, 1.5, None, ALU.add))
                    ins = pool.tensor_tensor(y, y, u, ALU.mult)
                    if k < 2:
                        chain.link(ins)
                ins.then_inc(done, 1)
                chain.end()

            nwt, nwt2 = Chain(nwt_chain), Chain(nwt2_chain)

            def squares(n):
                pool.wait_ge(hT_done, n + 1)
                after(pool, guard_psum, n)
                pool.tensor_tensor(sq[:, :], h3[:, 0, :], h3[:, 0, :], ALU.mult).then_inc(sq_done, 1)

            def put_vals(b, t):
                apart(pool, xs_done, b + 1)
                apart(pool, summed, (b - 1) * NG + t + 1)
                src = xs[:, :, :].rearrange("p i (h d) -> p i h d", d=HD)[:, :, HG * t:HG * t + HG, :]
                pool.tensor_copy(vals[:, :, HG * t:HG * t + HG, 0:HD], src).then_inc(vals_done, 1)

            def add(n, q):
                i, cc = divmod(q, CPT)
                if cc:
                    k = n * NT * (CPT - 1) + i * (CPT - 1) + cc - 1
                    pool.wait_ge(expert_used, n * CHUNKS + q + 1)
                    after(pool, added, k)
                    pool.tensor_tensor(acc[:, i], acc[:, i], gated[:, (i * (CPT - 1) + cc - 1) % 2],
                                       ALU.add).then_inc(added, 1)

            def body(b, tail, head, prep):
                for s in range(16):
                    if s == 0 and not (isinstance(b, int) and b == 0):
                        put_vals(b, NG - 2)
                    if s == 1 and prep:
                        newton(nwt, b + 1, nr, seeded, rstd_done)
                    if s == 4:
                        put_vals(b, NG - 1)
                    if s == 7 and prep:
                        squares(b + 1)
                    if s == 8 and head:
                        newton(nwt2, b - 1, nr2, seeded2, rstd2_done)
                    if s == 9 and prep:
                        put_vals(b + 1, 0)
                    if s == 12 and prep:
                        put_vals(b + 1, 1)
                    if tail:
                        for q in tail_chunks[s]:
                            add(b - 2, q)
                    if head:
                        for q in head_chunks[s]:
                            add(b - 1, q)

            newton(nwt, 0, nr, seeded, rstd_done)
            squares(0)
            stack_consts()
            for t in range(NG - 1):
                put_vals(0, t)
            schedule(pool, body)
            for q in range(HEAD_N, CHUNKS):
                add(B - 2, q)
            newton(nwt2, B - 1, nr2, seeded2, rstd2_done)
            for q in range(CHUNKS):
                add(B - 1, q)

        @block.scalar
        def _(act):
            act.dma_start(c_in[:, :], c).then_inc(small_in, 16)
            act.dma_start(rw_in[:, :], router_w).then_inc(small_in, 16)
            act.dma_start(wcol[:, 0:1], bass.AP(ipw.tensor, 0, [[0, P], [1, 1]])).then_inc(small_in, 16)
            act.wait_ge(small_in, 48)
            act.activation(wcol[:, 1:2], wcol[:, 0:1], ACT.Exp, scale=-1.0).then_inc(act_set, 1)
            act.wait_ge(dve_set, 1)
            act.activation(c_exp[:, :], cT[:, :], ACT.Exp, scale=-1.0).then_inc(act_set, 1)

            def h_out(n):
                act.wait_ge(hT_turned, n + 1)
                after(act, split_done, n)
                after(act, sq_done, n)
                after(act, guard_psum, n)
                act.activation(h3[:, 0, :], ps[:, TURN, :], ACT.Identity, bias=modT[:, 0, bass.ds(n, 1)],
                               scale=modT[:, 1, bass.ds(n, 1)]).then_inc(hT_done, 1)

            def first_parts(n):
                act.wait_ge(scaled_done, n + 1)
                after(act, stored, n * STORES)
                act.activation(parts[:, :, 0, :], h3[:, :, :], ACT.Copy).then_inc(hi_done, 1)

            def second_parts(n):
                act.wait_ge(hres_done, n + 1)
                act.activation(parts[:, :, 1, :], hres[:, :, :], ACT.Copy).then_inc(mid_done, 1)

            def guard_first(n):
                act.wait_ge(guard_read, n + 1)
                act.activation(g_parts[:, 0, :], g_neg[:, :], ACT.Copy).then_inc(g_hi_done, 1)

            def guard_second(n):
                act.wait_ge(g_res_done, n + 1)
                act.activation(g_parts[:, 1, :], g_res[:, :], ACT.Copy).then_inc(g_mid_done, 1)

            def gate_row(n):
                k, half = divmod(n, 2)
                act.wait_ge(rows_done, n + 1)
                src = ps[:, EXPERT + n % 2, :].rearrange("p (b d) -> p b d", d=D)
                act.activation(gate_rows[:, k, 4 * half:4 * half + 4, :], src, ACT.Copy).then_inc(act_set, 1)

            def h2_out(n):
                act.wait_ge(h2_turned, n + 1)
                after(act, expert, n * CHUNKS)
                act.activation(h2[:, :], ps[:, TURN, :], ACT.Identity, bias=modT[:, 3, bass.ds(n, 1)],
                               scale=modT[:, 4, bass.ds(n, 1)]).then_inc(h2_done, 1)

            def router_exp(n):
                act.wait_ge(lgt_done, n + 1)
                act.activation(pex[:, :, :], lgt[:, :, :], ACT.Exp).then_inc(pex_done, 1)

            def sums_copy(g):
                act.wait_ge(summed, g + 1)
                after(act, sums_turned, g)
                act.activation(o_sb[:, :], ps[:, SUMS, :], ACT.Copy).then_inc(sums_out, 1)

            def exps(b, t, hh):
                if hh == 0:
                    after(act, summed, b * NG + t - 1)
                for p in range(2):
                    u = t * UNITS + 2 * hh + p
                    act.wait_ge(scored, b * BU + u + 1)
                    bank = 2 * p
                    act.activation(probs[:, t % 2, hh, 2 * p:2 * p + 2, :], ps[:, bank:bank + 2, :],
                                   ACT.Exp, scale=SCALE).then_inc(expd, 1)

            def body(b, tail, head, prep):
                for s in range(16):
                    t, hh = divmod(s, HG)
                    first = isinstance(b, int) and b * NG + t < 2
                    if hh == 0 and not first:
                        sums_copy(b * NG + t - 2)
                    exps(b, t, hh)
                    if s == 6 and prep:
                        h_out(b + 1)
                    if s == 8 and prep:
                        first_parts(b + 1)
                    if s == 9 and prep:
                        guard_first(b + 1)
                        second_parts(b + 1)
                    if s == 10 and prep:
                        guard_second(b + 1)
                    if s == 10 and head:
                        h2_out(b - 1)
                    if s == 12 and head:
                        router_exp(b - 1)
                    if ROWS_AT <= s < ROWS_AT + 6 and isinstance(b, int) and b == 0:
                        gate_row(s - ROWS_AT)

            act.wait_ge(dve_set, 4)
            h_out(0)
            first_parts(0)
            second_parts(0)
            guard_first(0)
            guard_second(0)
            schedule(act, body)
            sums_copy(B * NG - 2)
            sums_copy(B * NG - 1)
            h2_out(B - 1)
            router_exp(B - 1)

        @block.vector
        def _(dve):
            n_setup = [0]

            def link(ins):
                n_setup[0] += 1
                ins.then_inc(dve_chain, 1)
                dve.wait_ge(dve_chain, n_setup[0])

            prep_c, res_c, gate_c, fin_c = Chain(prep_chain), Chain(res_chain), Chain(gate_chain), Chain(fin_chain, per=3)

            def moments(chain, src, stats, mv, nrt, seeded_s):
                for i in range(NT):
                    ins = dve.bn_stats(stats[:, i, :], src[:, i, :])
                chain.link(ins, alone=True)
                for i in range(NT):
                    ins = dve.bn_aggr(mv[:, i, :], stats[:, i, :])
                chain.link(ins)
                chain.link(dve.tensor_scalar(nrt[:, 0, :], mv[:, :, 1], LN_EPS, None, ALU.add))
                dve.tensor_scalar(nrt[:, 1, :], nrt[:, 0, :], -0.5, None, ALU.mult)
                chain.link(dve.tensor_scalar(nrt[:, 4, :].bitcast(I32), nrt[:, 0, :].bitcast(I32), 1, None,
                                             ALU.arith_shift_right))
                dve.tensor_scalar(nrt[:, 2, :].bitcast(I32), nrt[:, 4, :].bitcast(I32), -1.0,
                                  float(0x5F3759DF), ALU.mult, ALU.add).then_inc(seeded_s, 1)

            def normalise(dst, src, mv, nrt, done):
                for i in range(NT):
                    ins = dve.tensor_scalar(dst[:, i, :], src[:, i, :], mv[:, i, 0:1], nrt[:, 2, i:i + 1],
                                            ALU.subtract, ALU.mult)
                ins.then_inc(done, 1)

            def prep_ln(n):
                prep_c.start(dve, n)
                moments(prep_c, xt[:, n], stats, mv, nr, seeded)

            def prep_xs(n):
                dve.wait_ge(rstd_done, n + 1)
                after(dve, vals_done, n * NG)
                after(dve, hT_turned, n)
                prep_c.end()
                normalise(xs, xt[:, n], mv, nr, xs_done)

            def scale_h(n):
                dve.wait_ge(hT_done, n + 1)
                dve.tensor_scalar(h3[:, 1, :], h3[:, 0, :], wcol[:, 2:3], None, ALU.mult)
                dve.tensor_scalar(h3[:, 2, :], h3[:, 0, :], wcol[:, 3:4], None, ALU.mult).then_inc(scaled_done, 1)

            def first_rest(n):
                dve.wait_ge(hi_done, n + 1)
                dve.tensor_tensor(hres[:, :, :], h3[:, :, :], parts[:, :, 0, :], ALU.subtract).then_inc(hres_done, 1)

            def third_parts(n):
                dve.wait_ge(mid_done, n + 1)
                dve.tensor_tensor(parts[:, :, 2, :], hres[:, :, :], parts[:, :, 1, :],
                                  ALU.subtract).then_inc(split_done, 1)

            def true_max(n):
                with dve.Fori(0, HEADS) as h:
                    dve.tensor_scalar(h_one[:, :], h3[:, 0, :], head_sel[:, bass.ds(h, 1)], None,
                                      ALU.mult).then_inc(one_done, 1)
                    for i in range(NT):
                        k = n * HEADS * NT + h * NT + i
                        dve.wait_ge(one_score, k + 1)
                        src = ps[:, EXPERT + 1, :].rearrange("p (r j) -> p r j", r=RES)
                        dve.tensor_reduce(blk[:, 0, :], src, AX_X, ALU.max).then_inc(one_used, 1)
                        dve.wait_ge(one_used, 3 * k + 1)
                        dve.tensor_tensor(blk[:, 1, :], blk[:, 0, :], mask_w[:, i, :],
                                          ALU.mult).then_inc(one_used, 1)
                        dve.wait_ge(one_used, 3 * k + 2)
                        dve.tensor_reduce(rowmax[:, i, bass.ds(h, 1)], blk[:, 1, :], AX_X,
                                          ALU.max).then_inc(one_used, 1)
                        dve.wait_ge(one_used, 3 * k + 3)
                dve.engine_nop().then_inc(rowmax_done, 1)

            def guard_out(n):
                dve.wait_ge(guard_psum, n + 1)
                dve.tensor_scalar(g_neg[:, :], ps[0:HEADS, TURN, :], -1.0, None, ALU.mult).then_inc(guard_read, 1)

            def guard_rest(n):
                dve.wait_ge(g_hi_done, n + 1)
                dve.tensor_tensor(g_res[:, :], g_neg[:, :], g_parts[:, 0, :], ALU.subtract).then_inc(g_res_done, 1)

            def guard_third(n):
                dve.wait_ge(g_mid_done, n + 1)
                dve.tensor_tensor(g_parts[:, 2, :], g_res[:, :], g_parts[:, 1, :],
                                  ALU.subtract).then_inc(guard_done, 1)

            def finish_group(g, t):
                dve.wait_ge(sums_turned, g + 1)
                src = ps[:, TURN, :].rearrange("p (i h v) -> p i h v", i=NT, v=VW)
                dve.reciprocal(rden[:, :, :], src[:, :, :, HD]).then_inc(den_chain, 1)
                dve.wait_ge(den_chain, g + 1)
                dve.tensor_tensor(att[:, :, HG * t:HG * t + HG, :], src[:, :, :, 0:HD],
                                  rden[:, :, :].unsqueeze(3).to_broadcast([P, NT, HG, HD]),
                                  ALU.mult).then_inc(att_done, 1)

            def rows(k, n):
                return gate_rows[:, k, bass.ds(n, 1), :].to_broadcast([P, NT, D])

            def residual(n):
                dve.wait_ge(att_done, (n + 1) * NG)
                res_c.start(dve, n)
                res_c.link(dve.tensor_tensor(x2a[:, :, :], att[:, :, :, :].rearrange("p i h d -> p i (h d)"),
                                             rows(0, n), ALU.mult))
                res_c.link(dve.tensor_tensor(x2b[:, :, :], x2a[:, :, :], rows(1, n), ALU.add))
                res_c.link(dve.tensor_tensor(xt[:, n], xt[:, n], x2b[:, :, :], ALU.add), alone=True)

            def second_moments(n):
                moments(res_c, xt[:, n], stats2, mv2, nr2, seeded2)

            def second_ln(n):
                dve.wait_ge(rstd2_done, n + 1)
                after(dve, h2_turned, n)
                normalise(xs2, xt[:, n], mv2, nr2, xs2_done)
                res_c.end()

            def wide(t_, n_=E):
                return t_.unsqueeze(2).to_broadcast([P, NT, n_])

            def router(n):
                dve.wait_ge(logits, n + 1)
                gate_c.start(dve, n)
                lp = ps[:, TURN, 0:NT * E].rearrange("p (i e) -> p i e", e=E)
                dve.tensor_tensor(lgt[:, :, :], lp, rb[:, :].unsqueeze(1).to_broadcast([P, NT, E]),
                                  ALU.add).then_inc(logits_read, 1)
                dve.wait_ge(logits_read, n + 1)
                gate_c.link(dve.tensor_reduce(lmx[:, :], lgt[:, :, :], AX_X, ALU.max))
                dve.tensor_tensor(lgt[:, :, :], lgt[:, :, :], wide(lmx[:, :]), ALU.subtract).then_inc(lgt_done, 1)

            def router_gates(n):
                dve.wait_ge(pex_done, n + 1)
                gate_c.link(dve.tensor_reduce(pz[:, 0, :], pex[:, :, :], AX_X, ALU.add))
                gate_c.link(dve.reciprocal(pz[:, 1, :], pz[:, 0, :]))
                gate_c.link(dve.tensor_tensor(prb[:, :, 0:E], pex[:, :, :], wide(pz[:, 1, :]), ALU.mult), alone=True)
                for i in range(NT):
                    ins = dve.max(top8[:, i, :], prb[:, i, 0:E])
                gate_c.link(ins)
                gate_c.link(dve.tensor_copy(top8[:, :, TOPK:8], prb[:, :, E:E + 2]), alone=True)
                for i in range(NT):
                    ins = dve.match_replace(rest[:, i, :], top8[:, i, :], prb[:, i, :], 0.0)
                gate_c.link(ins)
                gate_c.link(dve.tensor_tensor(gsel[:, :, :], prb[:, :, 0:E], rest[:, :, 0:E], ALU.subtract))
                gate_c.link(dve.tensor_reduce(pz[:, 2, :], gsel[:, :, :], AX_X, ALU.add))
                gate_c.link(dve.tensor_scalar(pz[:, 2, :], pz[:, 2, :], FFN_EPS, None, ALU.add))
                gate_c.link(dve.reciprocal(pz[:, 3, :], pz[:, 2, :]))
                gate_c.link(dve.tensor_tensor(gate[:, :, :], gsel[:, :, :], wide(pz[:, 3, :]), ALU.mult))
                gate_c.link(dve.tensor_reduce(pz[:, 4, :], gate[:, :, :], AX_X, ALU.add))
                dve.tensor_scalar(eps_row[:, :], pz[:, 4, :], FFN_EPS, None, ALU.mult)
                gate_c.link(dve.tensor_scalar(pz[:, 5, :], pz[:, 4, :], FFN_EPS, None, ALU.max))
                gate_c.link(dve.reciprocal(pz[:, 0, :], pz[:, 5, :]))
                gate_c.link(dve.tensor_tensor(gate_n[:, :, :], gate[:, :, :], wide(pz[:, 0, :]), ALU.mult))
                gate_c.end()

            def experts(n, q):
                i, cc = divmod(q, CPT)
                k = i * (CPT - 1) + cc - 1
                dve.wait_ge(expert, n * CHUNKS + q + 1)
                if cc:
                    after(dve, added, n * NT * (CPT - 1) + k - 1)
                dst = gated[:, k % 2] if cc else acc[:, i]
                src = ps[:, EXPERT + q % 2, :].rearrange("p (e d) -> p e d", d=D)
                g = gate_n[:, i, CE * cc:CE * cc + CE].unsqueeze(2).to_broadcast([P, CE, D])
                dve.tensor_tensor(dst, src, g, ALU.mult).then_inc(expert_used, 1)

            def finish_sums(n):
                dve.wait_ge(added, (n + 1) * NT * (CPT - 1))
                fin_c.start(dve, n)
                fin_c.link(dve.tensor_tensor(acc2[:, :, :, :], acc[:, :, 0:2, :], acc[:, :, 2:4, :], ALU.add))
                for i in range(NT):
                    ins = dve.scalar_tensor_tensor(x2a[:, i, :], acc2[:, i, 0, :], eps_row[:, i:i + 1],
                                                   acc2[:, i, 1, :], ALU.add, ALU.add)
                fin_c.link(ins)

            def finish(n):
                fin_c.link(dve.tensor_tensor(x2b[:, :, :], x2a[:, :, :], rows(2, n), ALU.mult))
                dve.tensor_tensor(xt[:, n], xt[:, n], x2b[:, :, :], ALU.add).then_inc(y_done, 1)
                dve.wait_ge(y_done, n + 1)
                fin_c.end()

            dve.memset(qry_w[:, :, :, :].bitcast(F32), 0.0).then_inc(zeroed, 1)
            dve.memset(qry_c[:, :, :, :].bitcast(F32), 0.0).then_inc(zeroed, 1)
            dve.memset(vals[:, :, :, :], 0.0).then_inc(zeroed, 1)
            dve.memset(own[:, :, :], 0.0).then_inc(dve_chain, 1)
            dve.memset(prb[:, :, E:E + 1], -1.0).then_inc(dve_chain, 1)
            dve.memset(prb[:, :, E + 1:E + 2], -2.0).then_inc(dve_chain, 1)
            n_setup[0] = 3
            dve.wait_ge(dve_chain, 3)
            for i in range(NT):
                dve.memset(own[0:RB, i, 2 * i:2 * i + 1], 1.0)
                ins = dve.memset(own[RB:P, i, 2 * i + 1:2 * i + 2], 1.0)
            link(ins)
            dve.wait_ge(pe_set, 1)
            dve.tensor_copy(cT[:, :], ps[:, TURN, 0:B]).then_inc(dve_set, 1)
            link(dve.tensor_copy(rwT[:, :], ps[:, TURN, B:B + E]))
            dve.wait_ge(act_set, 2)
            link(dve.tensor_scalar(c_exp[:, :], c_exp[:, :], 1.0, None, ALU.add))
            link(dve.reciprocal(c_exp[:, :], c_exp[:, :]))
            dve.tensor_tensor(siluT[:, :], cT[:, :], c_exp[:, :], ALU.mult).then_inc(dve_set, 1)
            link(dve.tensor_scalar(wcol[:, 1:2], wcol[:, 1:2], 1.0, None, ALU.add))
            link(dve.reciprocal(wcol[:, 2:3], wcol[:, 1:2]))
            link(dve.tensor_scalar(wcol[:, 3:4], wcol[:, 2:3], -1.0, 1.0, ALU.mult, ALU.add))
            dve.tensor_scalar(mask_w[:, :, :], own[:, :, :], wcol[:, 3:4], wcol[:, 2:3], ALU.mult,
                              ALU.add).then_inc(dve_set, 1)
            dve.wait_ge(x0_in, 32)
            prep_ln(0)
            prep_xs(0)
            dve.wait_ge(pe_set, 2)
            link(dve.tensor_copy(modT[:, :, :], ps[:, EXPERT, 0:6 * B].rearrange("p (k b) -> p k b", b=B)))
            link(dve.tensor_scalar(modT[:, 1, :], modT[:, 1, :], 1.0, None, ALU.add))
            dve.tensor_scalar(modT[:, 4, :], modT[:, 4, :], 1.0, None, ALU.add).then_inc(dve_set, 1)
            dve.wait_ge(dve_set, 4)
            dve.tensor_reduce(bound[:, 0:1], modT[:, 1, :], AX_X, ALU.max, apply_absolute_value=True)
            dve.tensor_reduce(bound[:, 1:2], modT[:, 0, :], AX_X, ALU.max,
                              apply_absolute_value=True).then_inc(dve_set, 1)
            for k, col in ((0, 2), (1, 5)):
                dst = gates[:, 2 * k, :]
                link(dve.tensor_scalar(gate_tmp[:, 0, :], modT[:, col, :], 0.0, 2.0, ALU.is_ge, ALU.mult))
                link(dve.tensor_scalar(gate_tmp[:, 1, :], modT[:, col, :], -1.0, None, ALU.mult))
                link(dve.tensor_tensor(gate_tmp[:, 1, :], gate_tmp[:, 1, :], modT[:, col, :], ALU.max))
                link(dve.tensor_scalar(gate_tmp[:, 1, :], gate_tmp[:, 1, :], 0.25, None, ALU.max))
                link(dve.scalar_tensor_tensor(dst, gate_tmp[:, 0, :], -1.0, gate_tmp[:, 1, :], ALU.add, ALU.mult))
            link(dve.tensor_tensor(gates[:, 1, :], gates[:, 0, :], modT[:, 0, :], ALU.mult))
            link(dve.tensor_tensor(gates[:, 0, :], gates[:, 0, :], modT[:, 1, :], ALU.mult))
            dve.wait_ge(pe_set, 3)
            link(dve.tensor_reduce(bound1[:, 0:2], ps[0:1, EXPERT + 1, 0:2 * P].rearrange("p (k n) -> p k n", k=2),
                                   AX_X, ALU.max))
            link(dve.tensor_scalar(bound1[:, 2:3], bound1[:, 0:1], float(D) ** 0.5, None, ALU.mult))
            link(dve.scalar_tensor_tensor(bound1[:, 3:4], bound1[:, 1:2], float(HD) ** 0.5, bound1[:, 2:3],
                                          ALU.mult, ALU.add))
            dve.tensor_scalar(unsafe[:, :], bound1[:, 3:4], bound1[:, 3:4], float(SAFE_NORM2), ALU.mult,
                              ALU.is_gt).then_inc(flag_set, 1)
            dve.wait_ge(flag_set, 1)
            unsafe_v = dve.value_load(unsafe[0:1, 0:1], min_val=0, max_val=1)

            def diagonal(n):
                k, half = divmod(n, 2)
                after(dve, rows_done, n - 1)
                dve.tensor_tensor(acc[:, n % 2, :, :], ident[:, :].unsqueeze(1).to_broadcast([P, 4, P]),
                                  gates[:, k, 4 * half:4 * half + 4].unsqueeze(2).to_broadcast([P, 4, P]),
                                  ALU.mult).then_inc(diag_set, 1)

            def guard(n):
                with dve.If(unsafe_v):
                    true_max(n)

            scale_h(0)
            guard(0)
            guard_out(0)
            first_rest(0)
            third_parts(0)
            guard_rest(0)
            guard_third(0)
            dve.wait_ge(x1_in, 32)

            def body(b, tail, head, prep):
                for s in range(16):
                    t, hh = divmod(s, HG)
                    first = isinstance(b, int) and b * NG + t < 2
                    if hh == 2 and not first:
                        finish_group(b * NG + t - 2, (t - 2) % NG)
                    if s == 0 and prep:
                        prep_ln(b + 1)
                    if s == 5 and prep:
                        prep_xs(b + 1)
                    if s == 6 and head:
                        residual(b - 1)
                    if s == 7 and head:
                        second_moments(b - 1)
                    if s == 8 and prep:
                        scale_h(b + 1)
                        guard(b + 1)
                    if s == 9 and prep:
                        first_rest(b + 1)
                        guard_out(b + 1)
                    if s == 9 and head:
                        second_ln(b - 1)
                    if s == 10 and prep:
                        third_parts(b + 1)
                        guard_rest(b + 1)
                    if s == 11 and prep:
                        guard_third(b + 1)
                    if s == 11 and tail:
                        finish_sums(b - 2)
                    if s == 12 and head:
                        router(b - 1)
                    if s == 12 and tail:
                        finish(b - 2)
                    if s == 13 and head:
                        router_gates(b - 1)
                    if tail:
                        for q in tail_chunks[s]:
                            experts(b - 2, q)
                    if head:
                        for q in head_chunks[s]:
                            experts(b - 1, q)
                    if ROWS_AT <= s < ROWS_AT + 6 and isinstance(b, int) and b == 0:
                        diagonal(s - ROWS_AT)
                    if s == 15 and isinstance(b, int) and b == 0:
                        dve.wait_ge(x_in, 32 * (B - 2))
                        dve.wait_ge(act_set, 8)
                        dve.wait_ge(rows_done, 6)
                        dve.wait_ge(rb_in, 16)

            schedule(dve, body)
            for q in range(HEAD_N, CHUNKS):
                experts(B - 2, q)
            finish_sums(B - 2)
            finish(B - 2)
            finish_group(B * NG - 2, NG - 2)
            finish_group(B * NG - 1, NG - 1)
            residual(B - 1)
            second_moments(B - 1)
            second_ln(B - 1)
            router(B - 1)
            router_gates(B - 1)
            for q in range(CHUNKS):
                experts(B - 1, q)
            finish_sums(B - 1)
            finish(B - 1)

        @block.tensor
        def _(pe):
            mm = pe.matmul

            def turn4(src, done):
                for i in range(NT):
                    ins = pe.transpose(ps[:, TURN, i * P:(i + 1) * P], src(i), ident[:, :])
                ins.then_inc(done, 1)

            def prep_turn(n):
                pe.wait_ge(xs_done, n + 1)
                turn4(lambda i: xs[:, i, :], hT_turned)

            def prep_guard(n):
                with pe.If(unsafe_v):
                    with pe.Fori(0, HEADS) as h:
                        pe.wait_ge(one_done, n * HEADS + h + 1)
                        for i in range(NT):
                            k = n * HEADS * NT + h * NT + i
                            if i:
                                pe.wait_ge(one_used, 3 * k)
                            mm(ps[:, EXPERT + 1, :], h_one[:, i * P:(i + 1) * P], h3[:, 0, :], start=True,
                               stop=True).then_inc(one_score, 1)
                    pe.wait_ge(rowmax_done, n + 1)
                    for i in range(NT):
                        ins = pe.transpose(ps[0:HEADS, TURN, i * P:(i + 1) * P], rowmax[:, i, :], ident[:, :])
                    ins.then_inc(guard_psum, 1)
                with pe.Else():
                    pe.wait_ge(sq_done, n + 1)
                    mm(ps[0:HEADS, TURN, :], head_sel[:, :], sq[:, :], start=True,
                       stop=True).then_inc(guard_psum, 1)

            def scores(b, t, hh):
                if hh == 0:
                    pe.wait_ge(loaded[t % 2], (b * 2 + t // 2 + 1) * 8 * 16)
                for p in range(2):
                    u = t * UNITS + 2 * hh + p
                    after(pe, expd, b * BU + u - 1)
                    for i in (2 * p, 2 * p + 1):
                        lo, sl = i * P, t % 2
                        mm(ps[:, i, :], keys[:, sl, hh, lo:lo + P], qry_w[:, sl, hh, :], start=True, stop=False,
                           skip_group_check=True)
                        for r in range(2):
                            at = lo + r * RB
                            ins = mm(ps[r * RB:(r + 1) * RB, i, at:at + RB], keys[:, sl, hh, at:at + RB],
                                     qry_c[:, sl, hh, at:at + RB], start=False, stop=True, skip_group_check=True)
                    ins.then_inc(scored, 1)

            def sums(g, t, i):
                if i == 0:
                    pe.wait_ge(vals_done, g + 1)
                    pe.wait_ge(expd, (g + 1) * UNITS)
                    after(pe, sums_out, g)
                for hh in range(HG):
                    ins = mm(ps[VW * hh:VW * hh + VW, SUMS, :], vals[:, i, HG * t + hh, :],
                             probs[:, t % 2, hh, i, :], start=(i == 0), stop=(i == NT - 1), skip_group_check=True)
                if i == NT - 1:
                    ins.then_inc(summed, 1)

            def sums_turn(g):
                pe.wait_ge(sums_out, g + 1)
                turn4(lambda i: o_sb[:, i * P:(i + 1) * P], sums_turned)

            def h2_turn(n):
                pe.wait_ge(xs2_done, n + 1)
                turn4(lambda i: xs2[:, i, :], h2_turned)

            def route(n):
                pe.wait_ge(h2_done, n + 1)
                for i in range(NT):
                    ins = mm(ps[:, TURN, i * E:(i + 1) * E], h2[:, i * P:(i + 1) * P], rwT[:, :], start=True, stop=True)
                ins.then_inc(logits, 1)

            def experts(n, q):
                i, cc = divmod(q, CPT)
                after(pe, expert_used, n * CHUNKS + q - 1)
                mm(ps[:, EXPERT + q % 2, :], h2[:, i * P:(i + 1) * P], we[:, CE * cc:CE * cc + CE, :], start=True,
                   stop=True).then_inc(expert, 1)

            pe.wait_ge(pool_set, 4)
            pe.wait_ge(small_in, 48)
            pe.transpose(ps[:, TURN, 0:B], c_in[:, :], ident[0:B, 0:B])
            pe.transpose(ps[:, TURN, B:B + E], rw_in[:, :], ident[0:E, 0:E]).then_inc(pe_set, 1)
            pe.wait_ge(consts_in, 16)
            pe.wait_ge(dve_set, 2)
            for k in range(6):
                ins = mm(ps[:, EXPERT, k * B:(k + 1) * B], wmod_sb[:, k * D:(k + 1) * D], siluT[:, :],
                         start=True, stop=True)
            ins.then_inc(pe_set, 1)
            prep_turn(0)
            pe.wait_ge(dve_set, 5)
            for k in range(2):
                ins = pe.transpose(ps[0:1, EXPERT + 1, k * P:(k + 1) * P], bound[:, k:k + 1], ident[:, :])
            ins.then_inc(pe_set, 1)
            pe.wait_ge(flag_set, 1)
            unsafe_v = pe.value_load(unsafe[0:1, 0:1], min_val=0, max_val=1)
            pe.wait_ge(hT_done, 1)
            pe.wait_ge(pool_set, 6)
            prep_guard(0)
            pe.wait_ge(zeroed, 3)
            pe.wait_ge(pool_set, 9)

            def gate_row(n):
                pe.wait_ge(diag_set, n + 1)
                after(pe, act_set, 2 + n - 1)
                mm(ps[:, EXPERT + n % 2, :], ones[:, :], acc[:, n % 2, :, :], start=True,
                   stop=True).then_inc(rows_done, 1)

            def body(b, tail, head, prep):
                for s in range(16):
                    t, hh = divmod(s, HG)
                    g = b * NG + t
                    scores(b, t, hh)
                    if not (isinstance(b, int) and g < 1):
                        sums(g - 1, (t - 1) % NG, hh)
                    if hh == 1 and not (isinstance(b, int) and g < 2):
                        if t < 2:
                            after(pe, att_done, g - 2)
                        elif t == 2:
                            pe.wait_ge(guard_read, b + 2) if prep else pe.wait_ge(att_done, b * NG)
                        elif head:
                            pe.wait_ge(logits_read, b)
                        else:
                            pe.wait_ge(att_done, g - 2)
                        sums_turn(g - 2)
                    if s == 6 and prep:
                        after(pe, att_done, b * NG)
                        prep_turn(b + 1)
                    if s == 8 and prep:
                        pe.wait_ge(hT_done, b + 2)
                        prep_guard(b + 1)
                    if s == 10 and head:
                        pe.wait_ge(att_done, b * NG + 1)
                        h2_turn(b - 1)
                    if s == 11 and head:
                        route(b - 1)
                    if tail:
                        for q in tail_chunks[s]:
                            experts(b - 2, q)
                    if head:
                        for q in head_chunks[s]:
                            experts(b - 1, q)
                    if ROWS_AT <= s < ROWS_AT + 6 and isinstance(b, int) and b == 0:
                        gate_row(s - ROWS_AT)
                    if s == 15 and isinstance(b, int) and b == 0:
                        pe.wait_ge(act_set, 8)
                        pe.wait_ge(we_in, 16)

            schedule(pe, body)
            last = B * NG - 1
            for i in range(NT):
                sums(last, NG - 1, i)
            for q in range(HEAD_N, CHUNKS):
                experts(B - 2, q)
            pe.wait_ge(att_done, last - 1)
            sums_turn(last - 1)
            pe.wait_ge(att_done, last)
            sums_turn(last)
            pe.wait_ge(att_done, last + 1)
            h2_turn(B - 1)
            pe.wait_ge(h2_done, B)
            route(B - 1)
            for q in range(CHUNKS):
                experts(B - 1, q)


_INS = ["L0_attn_x", "L0_attn_inter_palace_weight", "L0_ffn_router_w", "L0_ffn_router_b", "L0_ffn_expert_w",
        "L0_c", "L0_wmod"]


def kernel(**inputs):
    import concourse.bacc as _bacc
    from concourse.bass_utils import run_bass_kernel_spmd as _run

    nc = _bacc.Bacc("TRN2", target_bir_lowering=False, num_devices=1)
    arrays, args = {}, []
    for name in _INS:
        a = np.ascontiguousarray(inputs[name])
        a = a.reshape(a.shape or (1,))
        arrays[f"in_{name}_dram"] = a
        args.append(nc.dram_tensor(f"in_{name}_dram", a.shape, mybir.dt.from_np(a.dtype), kind="ExternalInput").ap())
    shape = inputs["L0_attn_x"].shape
    out = nc.dram_tensor("out_0_dram", shape, F32, kind="ExternalOutput").ap()
    adaln_block(nc, *args, out)
    r = _run(nc, [arrays], core_ids=[0])
    return r.results[0]["out_0_dram"]
```

```python
from contextlib import ExitStack

import numpy as np
import concourse.bass as bass
from concourse import mybir

F32 = mybir.dt.float32
BF16 = mybir.dt.bfloat16
F16 = mybir.dt.float16
I32 = mybir.dt.int32
ALU = mybir.AluOpType
ACT = mybir.ActivationFunctionType
AX_X = mybir.AxisListType.X

P = 128
HEADS, HD = 16, 8
RES = 8
HG = 4
TOPK = 6
LN_EPS, FFN_EPS = 1e-5, 1e-10
SCALE = HD ** -0.5
VW = 32
SLOTS = [(0, 1), (0, 0), (0, 2), (1, 0), (1, 1), (2, 0)]
TOP = 14
EXPERT_PARTS = [(0, 0), (0, 1), (1, 0)]
ROWS = len(SLOTS) * HD
SAFE_NORM2 = 60 * 4 / SCALE


def adaln_block(nc, x, ipw, router_w, router_b, expert_w, c, wmod, out):
    B, T, D = x.shape
    E = expert_w.shape[0]
    NT = T // P
    NG = HEADS // HG
    UNITS = HG * NT // 2
    BU = NG * UNITS
    RB = T // RES
    CE = 4
    CPT = E // CE
    CHUNKS = NT * CPT
    assert D == P and T == 512 and NT == 4 and HEADS * HD == D

    TAIL = {0: 2, 1: 1, 2: 2, 3: 2, 4: 1, 5: 1, 6: 1, 7: 1, 8: 1, 10: 1}
    HEAD = {13: 1, 14: 1, 15: 1}
    HEAD_N = sum(HEAD.values())
    DRAIN_VEC = (11, 12, 13)
    VEC_PAIRS = (0, 1, 2, CHUNKS // 2 - 1)
    LAST_HEAD = {13: 1, 14: 2, 15: 2}
    DRAIN = [(B - 2, q) for q in range(sum(LAST_HEAD.values()), CHUNKS)] + [(B - 1, q) for q in range(CHUNKS)]

    def drain_on_vec(n, q):
        return q in DRAIN_VEC if n == B - 2 else q % CPT == 0 or q in (CPT - 1, CHUNKS - 1)

    def drained(n, q):
        on = drain_on_vec(n, q)
        upto = DRAIN[:DRAIN.index((n, q)) + 1]
        return on, sum(drain_on_vec(*c) == on for c in upto)
    assert HEAD_N + sum(TAIL.values()) == CHUNKS

    def tokens(t, b, half):
        return t[b].rearrange("(j i two) d -> two j i d", i=NT, two=2)[half]

    keys_scr = nc.dram_tensor("keys_scr", (B, HEADS, HD, len(SLOTS), T), BF16, kind="Internal").ap()
    qry_scr = nc.dram_tensor("qry_scr", (B, HEADS, HD, len(SLOTS), 2, T), BF16, kind="Internal").ap()
    guard_scr = nc.dram_tensor("guard_scr", (B, HEADS, 3, T), BF16, kind="Internal").ap()

    ctx = ExitStack()
    with ctx:
        def sb(name, shape, dt=F32):
            return ctx.enter_context(nc.sbuf_tensor(name, shape, dt))

        def sem(name):
            return ctx.enter_context(nc.semaphore(name))

        xt = sb("xt", [P, B, NT, D])
        ident = sb("ident", [P, P])
        ones = sb("ones", [P, P])
        head_sel = sb("head_sel", [P, HEADS])
        own = sb("own", [P, NT, RES])
        mask_w = sb("mask_w", [P, NT, RES])
        c_in = sb("c_in", [B, D])
        rw_in = sb("rw_in", [E, D])
        wmod_sb = sb("wmod_sb", [D, 6 * D])
        c_exp = sb("c_exp", [B, D])
        siluT = sb("siluT", [D, B])
        rwT = sb("rwT", [D, E])
        rb = sb("rb", [P, E])
        we = sb("we", [D, E, D])
        we_parts = sb("we_parts", [D, 2, E, D], F16)
        extent = sb("extent", [P, 3])
        ext1 = sb("ext1", [1, 8])
        ext_exp = sb("ext_exp", [1, 2], I32)
        scal1 = sb("scal1", [1, 6])
        scal = sb("scal", [P, 4])
        modT = sb("modT", [D, 6, B])
        gates = sb("gates", [D, 3, B])
        gate_sign = sb("gate_sign", [D, 2, B])
        gate_size = sb("gate_size", [D, 2, B])
        gate_rows = sb("gate_rows", [P, 3, B, D])
        wcol = sb("wcol", [P, 4])
        bound = sb("bound", [P, 2])
        bound1 = sb("bound1", [1, 4])
        unsafe = sb("unsafe", [1, 1], I32)

        stats = sb("stats", [P, NT, 6])
        mv = sb("mv", [P, NT, 2])
        stats2 = sb("stats2", [P, NT, 6])
        mv2 = sb("mv2", [P, NT, 2])
        nr = sb("nr", [P, 5, NT])
        xs = sb("xs", [P, NT, D])
        h3 = sb("h3", [D, 3, T])
        hres = sb("hres", [D, 3, T])
        parts = sb("parts", [D, 3, 3, T], BF16)
        sq = sb("sq", [D, T])
        g_neg = sb("g_neg", [HEADS, T])
        g_res = sb("g_res", [HEADS, T])
        g_parts = sb("g_parts", [HEADS, 3, T], BF16)
        h_one = sb("h_one", [D, T])
        blk = sb("blk", [P, 2, RES])
        rowmax = sb("rowmax", [P, NT, HEADS])

        keys = sb("keys", [P, 2, HG // 2, T], BF16)
        qry = sb("qry", [P, 2, HG // 2, 2, T], BF16)
        vals = sb("vals", [P, NT, HEADS, VW])
        probs = sb("probs", [P, 2, HG, NT, T])
        o_sb = sb("o_sb", [P, T])
        rden = sb("rden", [P, NT, HG])
        att = sb("att", [P, NT, HG, HD])
        att_step = sb("att_step", [P, NT, HG * HD])

        xs2 = sb("xs2", [P, NT, D])
        nr2 = sb("nr2", [P, 5, NT])
        ffn_row = sb("ffn_row", [P, NT, D])
        ffn_step = sb("ffn_step", [P, NT, D])
        lgt = sb("lgt", [P, NT, E])
        lmx = sb("lmx", [P, NT])
        pex = sb("pex", [P, NT, E])
        pz = sb("pz", [P, 6, NT])
        prb = sb("prb", [P, NT, E + 2])
        top8 = sb("top8", [P, NT, 8])
        rest = sb("rest", [P, NT, E + 2])
        gsel = sb("gsel", [P, NT, E])
        gate = sb("gate", [P, NT, E])
        h2_of = [sb("h2_last", [D, T]), sb("h2", [D, T])]
        h2_parts_of = [sb("h2_parts_last", [D, 2, T], F16), sb("h2_parts", [D, 2, T], F16)]
        gate_of = [sb("gate_last", [P, NT, E]), sb("gate_n", [P, NT, E])]
        eps_of = [sb("eps_last", [P, NT]), sb("eps_row", [P, NT])]
        acc = sb("acc", [P, NT, CE, D])
        gated = sb("gated", [P, 2, CE, D])
        acc2 = sb("acc2", [P, NT, 2, D])

        ps = ctx.enter_context(nc.psum_tensor("ps", [P, 8, T], F32))
        SUMS, TURN, EXPERT = 4, 5, 6

        consts_in = sem("consts_in")
        c_arrived = sem("c_arrived")
        small_in = sem("small_in")
        rb_in = sem("rb_in")
        x0_in = sem("x0_in")
        x1_in = sem("x1_in")
        zeroed = sem("zeroed")
        x_in = sem("x_in")
        we_in = sem("we_in")
        pool_set = sem("pool_set")
        dve_set = sem("dve_set")
        pe_set = sem("pe_set")
        act_set = sem("act_set")
        gates_set = sem("gates_set")
        dve_chain = sem("dve_chain")
        diag_set = sem("diag_set")
        rows_done = sem("rows_done")
        flag_set = sem("flag_set")
        prep_chain = sem("prep_chain")
        res_chain = sem("res_chain")
        gate_chain = sem("gate_chain")
        fin_chain = sem("fin_chain")
        den_chain = sem("den_chain")
        nwt_chain = sem("nwt_chain")
        nwt2_chain = sem("nwt2_chain")
        seeded = sem("seeded")
        rstd_done = sem("rstd_done")
        seeded2 = sem("seeded2")
        rstd2_done = sem("rstd2_done")
        xs_done = sem("xs_done")
        vals_done = sem("vals_done")
        hT_turned = sem("hT_turned")
        hT_done = sem("hT_done")
        sq_done = sem("sq_done")
        split_done = sem("split_done")
        guard_psum = sem("guard_psum")
        guard_read = sem("guard_read")
        guard_done = sem("guard_done")
        stored = sem("stored")
        guard_stored = sem("guard_stored")
        loaded = [sem("loaded0"), sem("loaded1")]
        scaled_done = sem("scaled_done")
        hi_done = sem("hi_done")
        hres_done = sem("hres_done")
        mid_done = sem("mid_done")
        g_hi_done = sem("g_hi_done")
        g_res_done = sem("g_res_done")
        g_mid_done = sem("g_mid_done")
        added = sem("added")
        one_done = sem("one_done")
        one_score = sem("one_score")
        one_used = sem("one_used")
        rowmax_done = sem("rowmax_done")
        scored = sem("scored")
        expd = sem("expd")
        summed = sem("summed")
        sums_out = sem("sums_out")
        sums_turned = sem("sums_turned")
        att_done = sem("att_done")
        based = sem("based")
        x2_done = sem("x2_done")
        xs2_done = sem("xs2_done")
        h2_turned = sem("h2_turned")
        h2_done = sem("h2_done")
        h2_hi_done = sem("h2_hi_done")
        h2_split = sem("h2_split")
        ext_set = sem("ext_set")
        ext_inv = sem("ext_inv")
        ext_turned = sem("ext_turned")
        we_hi_done = sem("we_hi_done")
        logits = sem("logits")
        logits_read = sem("logits_read")
        lgt_done = sem("lgt_done")
        pex_done = sem("pex_done")
        expert = sem("expert")
        expert_used = sem("expert_used")
        y_done = sem("y_done")
        pool_fin = sem("pool_fin")
        drain_vec = sem("drain_vec")
        drain_act = sem("drain_act")
        last_pair = sem("last_pair")
        last_y = sem("last_y")
        last_chain = sem("last_chain")
        y_out = sem("y_out")

        def after(eng, s, n):
            if not (isinstance(n, int) and n <= 0):
                eng.wait_ge(s, n)

        def apart(eng, s, n):
            after(eng, s, n)
            if not isinstance(n, int):
                eng.nop(nofuse=True)

        class Chain:
            def __init__(self, s, per=0):
                self.s, self.per = s, per

            def start(self, eng, n):
                self.eng, self.n, self.k = eng, n, 0

            def link(self, ins, alone=False):
                self.k += 1
                ins.then_inc(self.s, 1)
                (apart if alone else after)(self.eng, self.s, self.n * self.per + self.k)

            def end(self):
                assert self.per in (0, self.k)
                self.per = self.k

        def schedule(eng, body):
            body(0, tail=False, head=False, prep=True)
            body(1, tail=False, head=True, prep=True)
            with eng.Fori(2, B - 1) as b:
                body(b, tail=True, head=True, prep=True)
            body(B - 1, tail=True, head=True, prep=False)

        def chunk_list(table, base):
            out_, k = {}, base
            for s in range(16):
                out_[s] = list(range(k, k + table.get(s, 0)))
                k += table.get(s, 0)
            return out_
        head_chunks = chunk_list(HEAD, 0)
        last_head_chunks = chunk_list(LAST_HEAD, 0)
        tail_chunks = chunk_list(TAIL, HEAD_N)

        ROWS_EARLY = 3
        GATE_ROWS = {0: (3, 4, 5)}
        STORES = 16 * 2 * 3

        def rows(k, n):
            return gate_rows[:, k, bass.ds(n, 1), :].to_broadcast([P, NT, D])

        def drain_w(n):
            slot = (NG - 1) % 2 if n == B - 1 else (NG - 2) % 2
            return probs[:, slot].rearrange("p a b n -> p (a b n)").rearrange(
                "p (i c e d) -> p i c e d", i=NT, c=CPT, e=CE)

        last_w = drain_w(B - 1)

        def other(n):
            return 0 if isinstance(n, int) and n == B - 1 else 1

        DRAIN_BANKS = [0, 1, 2, 3, EXPERT, EXPERT + 1]

        def drain_bank(n, q):
            return DRAIN_BANKS[DRAIN.index((n, q)) % len(DRAIN_BANKS)]

        def wait_drained(eng, n, q):
            on, count = drained(n, q)
            eng.wait_ge(drain_vec if on else drain_act, count)

        def newton(eng, chain, n, nrt, seeded_s, done):
            eng.wait_ge(seeded_s, n + 1)
            chain.start(eng, n)
            y, u = nrt[:, 2, :], nrt[:, 3, :]
            for k in range(3):
                chain.link(eng.tensor_tensor(u, y, y, ALU.mult))
                chain.link(eng.tensor_tensor(u, u, nrt[:, 1, :], ALU.mult), alone=True)
                chain.link(eng.tensor_scalar(u, u, 1.5, None, ALU.add))
                ins = eng.tensor_tensor(y, y, u, ALU.mult)
                if k < 2:
                    chain.link(ins)
            ins.then_inc(done, 1)
            chain.end()

        block = ctx.enter_context(nc.Block())

        @block.sync
        def _(sp):
            def load_x(b, done):
                for half in range(2):
                    sp.dma_start(xt[half * RB:half * RB + RB, b, :, :], tokens(x, b, half)).then_inc(done, 16)

            load_x(0, x0_in)
            sp.dma_start(wmod_sb[:, :], wmod).then_inc(consts_in, 16)
            sp.dma_start(wcol[:, 0:1], bass.AP(ipw.tensor, 0, [[0, P], [1, 1]])).then_inc(small_in, 16)
            sp.dma_start(rw_in[:, :], router_w).then_inc(small_in, 16)

            def store(b):
                for part, done in enumerate((hi_done, mid_done, split_done)):
                    apart(sp, done, 3 * b + 1)
                    for dst, src, kind in ((keys_scr[b].rearrange("h d s n -> (h d) s n"), parts[:, part, 0, :], 0),
                                           (qry_scr[b].rearrange("h d s v n -> (h d) s (v n)"),
                                            parts[:, part, 1:3, :].rearrange("p v n -> p (v n)"), 1)):
                        at = [slot for slot, pair in enumerate(SLOTS) if pair[kind] == part]
                        step = at[1] - at[0] if len(at) > 1 else 1
                        if kind:
                            apart(sp, done, 3 * b + 3)
                        sp.dma_start(dst[:, at[0]:at[-1] + 1:step, :],
                                     src.unsqueeze(1).to_broadcast([P, len(at), src.shape[1]])).then_inc(stored, 16)

            def store_guard(b):
                apart(sp, guard_done, b + 1)
                sp.dma_start(guard_scr[b], g_parts[:, :, :]).then_inc(guard_stored, 16)

            def load(b, t):
                slot, heads = t % 2, slice(HG * t, HG * (t + 1))
                for half in range(2):
                    at = half * (P // 2)
                    k = keys_scr[b, heads].rearrange("(j two) d s n -> two (d s) j n", two=2)[half]
                    sp.dma_start(keys[at:at + ROWS, slot, :, :], k).then_inc(loaded[slot], 16)
                    q = qry_scr[b, heads].rearrange("(j two) d s v n -> two (d s) j (v n)", two=2)[half]
                    dst = qry[at:at + ROWS, slot, :, :, :].rearrange("p j v n -> p j (v n)")
                    sp.dma_start(dst, q).then_inc(loaded[slot], 16)

            def load_guard(b, t):
                slot, heads = t % 2, slice(HG * t, HG * (t + 1))
                for half in range(2):
                    at = half * (P // 2) + ROWS
                    g = guard_scr[b, heads].rearrange("(j two) a n -> two a j n", two=2)[half]
                    sp.dma_start(qry[at:at + 3, slot, :, 0, :], g).then_inc(loaded[slot], 16)

            def put_out(b):
                apart(sp, y_done, b + 1)
                for half in range(2):
                    sp.dma_start(tokens(out, b, half), xt[half * RB:half * RB + RB, b, :, :]).then_inc(y_out, 16)

            def body(b, tail, head, prep):
                for t in range(NG):
                    if t == 2 and prep:
                        store(b + 1)
                    apart(sp, scored, b * BU + (t + 1) * UNITS)
                    if t < 2:
                        load(b, t + 2)
                        load_guard(b, t + 2)
                    elif prep:
                        if t == 2:
                            apart(sp, stored, (b + 2) * STORES)
                        load(b + 1, t - 2)
                        if t == 2:
                            store_guard(b + 1)
                            apart(sp, guard_stored, 16 * (b + 2))
                        load_guard(b + 1, t - 2)
                    if t == 3 and tail:
                        put_out(b - 2)

            store(0)
            store_guard(0)
            sp.wait_ge(pool_set, 7)
            sp.wait_ge(zeroed, 1)
            sp.wait_ge(stored, STORES)
            load(0, 0)
            sp.wait_ge(guard_stored, 16)
            load_guard(0, 0)
            load(0, 1)
            load_guard(0, 1)
            load_x(1, x1_in)
            sp.dma_start(rb[:, :], bass.AP(router_b.tensor, 0, [[0, P], [1, E]])).then_inc(rb_in, 16)
            sp.dma_start(we[:, :, :], expert_w.rearrange("e d n -> d e n")).then_inc(we_in, 16)
            for b in range(2, B):
                load_x(b, x_in)
            schedule(sp, body)
            put_out(B - 2)
            for i in range(NT):
                sp.wait_ge(last_y, i + 1)
                for half in range(2):
                    sp.dma_start(tokens(out, B - 1, half)[:, i], xt[half * RB:half * RB + RB, B - 1, i, :]).then_inc(
                        y_out, 16)
            sp.wait_ge(y_out, 16 * 2 * (B - 1 + NT))

        @block.gpsimd
        def _(pool):
            def put(ins):
                ins.then_inc(pool_set, 1)
            put(pool.memset(ident[:, :], 0.0))
            put(pool.memset(ones[:, :], 1.0))
            put(pool.memset(head_sel[:, :], 1.0))
            pool.wait_ge(pool_set, 3)
            put(pool.affine_select(out=ident[:, :], in_=ident[:, :], compare_op=ALU.not_equal, fill=1.0,
                                   base=0, pattern=[[-1, P]], channel_multiplier=1))
            put(pool.affine_select(out=head_sel[:, :], in_=head_sel[:, :], compare_op=ALU.is_ge, fill=0.0,
                                   base=0, pattern=[[-HD, HEADS]], channel_multiplier=1))
            pool.wait_ge(pool_set, 5)
            put(pool.affine_select(out=head_sel[:, :], in_=head_sel[:, :], compare_op=ALU.is_ge, fill=0.0,
                                   base=HD - 1, pattern=[[HD, HEADS]], channel_multiplier=-1))

            put(pool.memset(keys[:, :, :, :], 1.0))
            put(pool.memset(vals[:, :, :, :], 0.0))

            nwt, nwt2 = Chain(nwt_chain, per=11), Chain(nwt2_chain)

            def squares(n):
                pool.wait_ge(hT_done, n + 1)
                after(pool, guard_psum, n)
                pool.tensor_tensor(sq[:, :], h3[:, 0, :], h3[:, 0, :], ALU.mult).then_inc(sq_done, 1)

            def guard_first(n):
                apart(pool, guard_read, n + 1)
                apart(pool, guard_stored, 16 * n)
                pool.tensor_copy(g_parts[:, 0, :], g_neg[:, :]).then_inc(g_hi_done, 1)

            def guard_second(n):
                apart(pool, g_res_done, n + 1)
                pool.tensor_copy(g_parts[:, 1, :], g_res[:, :]).then_inc(g_mid_done, 1)

            def put_vals(b, t):
                apart(pool, xs_done, b + 1)
                apart(pool, summed, (b - 1) * NG + t + 1)
                src = xs[:, :, :].rearrange("p i (h d) -> p i h d", d=HD)[:, :, HG * t:HG * t + HG, :]
                pool.tensor_copy(vals[:, :, HG * t:HG * t + HG, 0:HD], src).then_inc(vals_done, 1)

            def add(n, q):
                i, cc = divmod(q, CPT)
                if cc:
                    k = n * NT * (CPT - 1) + i * (CPT - 1) + cc - 1
                    pool.wait_ge(expert_used, n * CHUNKS + q + 1)
                    after(pool, added, k)
                    pool.tensor_tensor(acc[:, i], acc[:, i], gated[:, (i * (CPT - 1) + cc - 1) % 2],
                                       ALU.add).then_inc(added, 1)

            def body(b, tail, head, prep):
                for s in range(16):
                    if s == 0 and not (isinstance(b, int) and b == 0):
                        put_vals(b, NG - 2)
                    if s == 1 and prep:
                        newton(pool, nwt, b + 1, nr, seeded, rstd_done)
                    if s == 4:
                        put_vals(b, NG - 1)
                    if s == 7 and prep:
                        squares(b + 1)
                    if s == 8 and head:
                        newton(pool, nwt2, b - 1, nr2, seeded2, rstd2_done)
                    if s == 9 and prep:
                        put_vals(b + 1, 0)
                    if s == 10 and prep:
                        guard_first(b + 1)
                        base(b + 1)
                    if s == 11 and prep:
                        guard_second(b + 1)
                    if s == 12 and prep:
                        put_vals(b + 1, 1)
                    if s == 13 and isinstance(b, int) and b == 0:
                        pool.wait_ge(ext_set, 7)
                        pool.tensor_scalar(we_parts[:, 0].rearrange("p e d -> p (e d)"),
                                           we[:, :, :].rearrange("p e d -> p (e d)"), scal[:, 1:2], None,
                                           ALU.mult).then_inc(we_hi_done, 1)
                    if tail:
                        for q in tail_chunks[s]:
                            add(b - 2, q)
                    if head:
                        for q in (head_chunks if prep else last_head_chunks)[s]:
                            add(b - 1, q)

            def base(n):
                apart(pool, xs_done, n + 1)
                pool.tensor_tensor(xt[:, n], xt[:, n], rows(1, n), ALU.add).then_inc(based, 1)

            squares(0)
            pool.wait_ge(sq_done, 1)
            pool.wait_ge(pool_set, 8)
            put(pool.memset(vals[:, :, :, HD:HD + 1], 1.0))

            n_gates = [0]

            def link_gates(ins):
                n_gates[0] += 1
                ins.then_inc(gates_set, 1)
                pool.wait_ge(gates_set, n_gates[0])

            pool.wait_ge(dve_set, 4)
            pool.wait_ge(pool_set, 9)
            g_in, g_out = modT[:, 2:6:3, :], gates[:, 0:3:2, :]
            link_gates(pool.tensor_scalar(gate_sign[:, :, :], g_in, 0.0, 2.0, ALU.is_ge, ALU.mult))
            link_gates(pool.tensor_scalar(gate_sign[:, :, :], gate_sign[:, :, :], -1.0, None, ALU.add))
            link_gates(pool.tensor_tensor(gate_size[:, :, :], gate_sign[:, :, :], g_in, ALU.mult))
            link_gates(pool.tensor_scalar(gate_size[:, :, :], gate_size[:, :, :], 0.25, None, ALU.max))
            link_gates(pool.tensor_tensor(g_out, gate_sign[:, :, :], gate_size[:, :, :], ALU.mult))
            link_gates(pool.tensor_tensor(gates[:, 1, :], gates[:, 0, :], modT[:, 0, :], ALU.mult))
            link_gates(pool.tensor_tensor(gates[:, 0, :], gates[:, 0, :], modT[:, 1, :], ALU.mult))

            for n in range(6):
                k, half = divmod(n, 2)
                after(pool, rows_done, n - NT + 1)
                after(pool, diag_set, n)
                pool.tensor_tensor(acc[:, n % NT, :, :], ident[:, :].unsqueeze(1).to_broadcast([P, 4, P]),
                                   gates[:, k, 4 * half:4 * half + 4].unsqueeze(2).to_broadcast([P, 4, P]),
                                   ALU.mult).then_inc(diag_set, 1)
            for t in range(NG - 1):
                put_vals(0, t)
            pool.wait_ge(act_set, 8)
            base(0)
            schedule(pool, body)
            n = B - 2
            for q in range(DRAIN[0][1], CHUNKS):
                i, cc = divmod(q, CPT)
                if cc:
                    wait_drained(pool, n, q)
                    if (n, i * CPT) in DRAIN:
                        wait_drained(pool, n, i * CPT)
                    pool.wait_ge(added, n * NT * (CPT - 1) + i * (CPT - 1) + cc - 1)
                    pool.tensor_tensor(acc[:, i], acc[:, i], drain_w(n)[:, i, cc], ALU.add).then_inc(added, 1)

            def pair(k):
                i, cc = k // 2, 2 * (k % 2)
                wait_drained(pool, B - 1, CPT * i + cc)
                wait_drained(pool, B - 1, CPT * i + cc + 1)
                pool.tensor_tensor(last_w[:, i, cc], last_w[:, i, cc], last_w[:, i, cc + 1],
                                   ALU.add).then_inc(last_pair, 1)

            pool.wait_ge(added, (n + 1) * NT * (CPT - 1))
            pool.wait_ge(y_done, n)
            pool.tensor_tensor(acc2[:, :, :, :], acc[:, :, 0:2, :], acc[:, :, 2:4, :], ALU.add).then_inc(pool_fin, 1)
            pool.wait_ge(pool_fin, 1)
            pool.tensor_tensor(ffn_row[:, :, :], acc2[:, :, 0, :], acc2[:, :, 1, :], ALU.add).then_inc(pool_fin, 1)
            pool.wait_ge(pool_fin, 2)
            pool.tensor_tensor(ffn_row[:, :, :], ffn_row[:, :, :],
                               eps_of[1][:, :].unsqueeze(2).to_broadcast([P, NT, D]), ALU.add).then_inc(pool_fin, 1)
            pool.wait_ge(pool_fin, 3)
            pool.tensor_tensor(ffn_step[:, :, :], ffn_row[:, :, :], rows(2, n), ALU.mult).then_inc(pool_fin, 1)
            pool.wait_ge(pool_fin, 4)
            pool.tensor_tensor(xt[:, n], xt[:, n], ffn_step[:, :, :], ALU.add).then_inc(y_done, 1)
            pool.wait_ge(y_done, n + 1)
            for k in range(CHUNKS // 2):
                if k not in VEC_PAIRS:
                    pair(k)

        @block.scalar
        def _(act):
            act.dma_start(c_in[:, :], c).then_inc(c_arrived, 16)
            act.wait_ge(c_arrived, 16)
            act.activation(c_exp[:, :], c_in[:, :], ACT.Exp, scale=-1.0).then_inc(act_set, 1)
            act.wait_ge(small_in, 32)
            act.activation(wcol[:, 1:2], wcol[:, 0:1], ACT.Exp, scale=-1.0).then_inc(act_set, 1)

            def h_out(n):
                act.wait_ge(hT_turned, n + 1)
                after(act, split_done, 3 * n)
                after(act, sq_done, n)
                after(act, guard_psum, n)
                act.activation(h3[:, 0, :], ps[:, TURN, :], ACT.Identity, bias=modT[:, 0, bass.ds(n, 1)],
                               scale=modT[:, 1, bass.ds(n, 1)]).then_inc(hT_done, 1)

            def first_parts(n):
                after(act, stored, n * STORES)
                for k in range(3):
                    act.wait_ge(scaled_done, 2 * n + k) if k else act.wait_ge(hT_done, n + 1)
                    act.activation(parts[:, 0, k, :], h3[:, k, :], ACT.Copy).then_inc(hi_done, 1)

            def second_parts(n):
                for k in range(3):
                    act.wait_ge(hres_done, 3 * n + k + 1)
                    act.activation(parts[:, 1, k, :], hres[:, k, :], ACT.Copy).then_inc(mid_done, 1)

            def gate_row(n):
                k, half = divmod(n, 2)
                act.wait_ge(rows_done, n + 1)
                src = ps[:, EXPERT + n % 2, :].rearrange("p (b d) -> p b d", d=D)
                act.activation(gate_rows[:, k, 4 * half:4 * half + 4, :], src, ACT.Copy).then_inc(act_set, 1)

            def h2_out(n):
                act.wait_ge(h2_turned, n + 1)
                if other(n):
                    after(act, expert, n * CHUNKS)
                act.activation(h2_of[other(n)][:, :], ps[:, TURN, :], ACT.Identity, bias=modT[:, 3, bass.ds(n, 1)],
                               scale=modT[:, 4, bass.ds(n, 1)]).then_inc(h2_done, 1)

            def h2_first(n):
                act.wait_ge(h2_done, n + 1)
                act.activation(h2_parts_of[other(n)][:, 0, :], h2_of[other(n)][:, :], ACT.Copy).then_inc(h2_hi_done, 1)

            def router_exp(n):
                act.wait_ge(lgt_done, n + 1)
                act.activation(pex[:, :, :], lgt[:, :, :], ACT.Exp).then_inc(pex_done, 1)

            def sums_copy(g):
                act.wait_ge(summed, g + 1)
                after(act, sums_turned, g)
                act.activation(o_sb[:, :], ps[:, SUMS, :], ACT.Copy).then_inc(sums_out, 1)

            def exps(b, t, i):
                if i == 0:
                    after(act, summed, b * NG + t - 1)
                for j in range(2):
                    act.wait_ge(scored, b * BU + t * UNITS + 2 * i + j + 1)
                    act.activation(probs[:, t % 2, 2 * j:2 * j + 2, i, :], ps[:, 2 * j:2 * j + 2, :],
                                   ACT.Exp, scale=SCALE).then_inc(expd, 1)

            def body(b, tail, head, prep):
                for s in range(16):
                    t, hh = divmod(s, HG)
                    first = isinstance(b, int) and b * NG + t < 1
                    if hh == 1 and not first:
                        sums_copy(b * NG + t - 1)
                    if s == 13 and head:
                        router_exp(b - 1)
                    exps(b, t, hh)
                    if isinstance(b, int) and b == 0:
                        for n in GATE_ROWS.get(s, ()):
                            gate_row(n)
                    if s == 6 and prep:
                        h_out(b + 1)
                    if s == 8 and prep:
                        first_parts(b + 1)
                    if s == 9 and prep:
                        second_parts(b + 1)
                    if s == 10 and head:
                        h2_out(b - 1)
                    if s == 11 and head:
                        h2_first(b - 1)

            act.wait_ge(dve_set, 4)
            h_out(0)
            first_parts(0)
            second_parts(0)
            for src, part, ready, done in ((g_neg, 0, guard_read, g_hi_done), (g_res, 1, g_res_done, g_mid_done)):
                act.wait_ge(ready, 1)
                act.activation(g_parts[:, part, :], src[:, :], ACT.Copy).then_inc(done, 1)
            for n in range(ROWS_EARLY):
                gate_row(n)
            schedule(act, body)

            def gate_chunk(dst, n, q):
                i, cc = divmod(q, CPT)
                for e in range(CE):
                    at = CE * cc + e
                    ins = act.activation(dst[:, e, :], ps[:, drain_bank(n, q), e * D:(e + 1) * D], ACT.Copy,
                                         scale=gate_of[other(n)][:, i, at:at + 1])
                return ins

            def drain_chunk(n, q):
                i, cc = divmod(q, CPT)
                act.wait_ge(expert, n * CHUNKS + q + 1)
                dst = acc[:, i] if n == B - 2 and cc == 0 else drain_w(n)[:, i, cc]
                gate_chunk(dst, n, q).then_inc(drain_act, 1)

            sums_copy(B * NG - 1)
            act.wait_ge(expert_used, (B - 2) * CHUNKS + DRAIN[0][1])
            act.wait_ge(y_done, B - 2)
            mine = [c for c in DRAIN if not drain_on_vec(*c)]
            for n, q in mine:
                if n == B - 2 and q < DRAIN_VEC[0]:
                    drain_chunk(n, q)
            h2_out(B - 1)
            for n, q in mine:
                if n == B - 2 and q > DRAIN_VEC[0]:
                    if q == CHUNKS - 1:
                        router_exp(B - 1)
                    drain_chunk(n, q)
            wait_drained(act, B - 1, 0)
            for n, q in mine:
                if n == B - 1:
                    drain_chunk(n, q)

        @block.vector
        def _(dve):
            n_setup = [0]

            def link(ins):
                n_setup[0] += 1
                ins.then_inc(dve_chain, 1)
                dve.wait_ge(dve_chain, n_setup[0])

            prep_c, res_c, gate_c, fin_c = Chain(prep_chain), Chain(res_chain), Chain(gate_chain), Chain(fin_chain, per=3)

            def moments(chain, src, stats, mv, nrt, seeded_s):
                for i in range(NT):
                    ins = dve.bn_stats(stats[:, i, :], src[:, i, :])
                chain.link(ins, alone=True)
                for i in range(NT):
                    ins = dve.bn_aggr(mv[:, i, :], stats[:, i, :])
                chain.link(ins)
                chain.link(dve.tensor_scalar(nrt[:, 0, :], mv[:, :, 1], LN_EPS, None, ALU.add))
                dve.tensor_scalar(nrt[:, 1, :], nrt[:, 0, :], -0.5, None, ALU.mult)
                chain.link(dve.tensor_scalar(nrt[:, 4, :].bitcast(I32), nrt[:, 0, :].bitcast(I32), 1, None,
                                             ALU.arith_shift_right))
                dve.tensor_scalar(nrt[:, 2, :].bitcast(I32), nrt[:, 4, :].bitcast(I32), -1.0,
                                  float(0x5F3759DF), ALU.mult, ALU.add).then_inc(seeded_s, 1)

            def normalise(dst, src, mv, nrt, done):
                for i in range(NT):
                    ins = dve.tensor_scalar(dst[:, i, :], src[:, i, :], mv[:, i, 0:1], nrt[:, 2, i:i + 1],
                                            ALU.subtract, ALU.mult)
                ins.then_inc(done, 1)

            def prep_ln(n):
                prep_c.start(dve, n)
                moments(prep_c, xt[:, n], stats, mv, nr, seeded)

            def prep_xs(n):
                dve.wait_ge(rstd_done, n + 1)
                after(dve, vals_done, n * NG)
                after(dve, hT_turned, n)
                prep_c.end()
                normalise(xs, xt[:, n], mv, nr, xs_done)

            def scale_h(n):
                dve.wait_ge(hT_done, n + 1)
                for k in range(2):
                    dve.tensor_scalar(h3[:, 1 + k, :], h3[:, 0, :], wcol[:, 2 + k:3 + k], None,
                                      ALU.mult).then_inc(scaled_done, 1)

            def first_rest(n):
                for k in range(3):
                    dve.wait_ge(hi_done, 3 * n + k + 1)
                    dve.tensor_tensor(hres[:, k, :], h3[:, k, :], parts[:, 0, k, :],
                                      ALU.subtract).then_inc(hres_done, 1)

            def third_parts(n):
                for k in range(3):
                    dve.wait_ge(mid_done, 3 * n + k + 1)
                    dve.tensor_tensor(parts[:, 2, k, :], hres[:, k, :], parts[:, 1, k, :],
                                      ALU.subtract).then_inc(split_done, 1)

            def true_max(n):
                dve.wait_ge(pool_set, 6)
                with dve.Fori(0, HEADS) as h:
                    dve.tensor_scalar(h_one[:, :], h3[:, 0, :], head_sel[:, bass.ds(h, 1)], None,
                                      ALU.mult).then_inc(one_done, 1)
                    for i in range(NT):
                        k = n * HEADS * NT + h * NT + i
                        dve.wait_ge(one_score, k + 1)
                        src = ps[:, EXPERT + 1, :].rearrange("p (r j) -> p r j", r=RES)
                        dve.tensor_reduce(blk[:, 0, :], src, AX_X, ALU.max).then_inc(one_used, 1)
                        dve.wait_ge(one_used, 3 * k + 1)
                        dve.tensor_tensor(blk[:, 1, :], blk[:, 0, :], mask_w[:, i, :],
                                          ALU.mult).then_inc(one_used, 1)
                        dve.wait_ge(one_used, 3 * k + 2)
                        dve.tensor_reduce(rowmax[:, i, bass.ds(h, 1)], blk[:, 1, :], AX_X,
                                          ALU.max).then_inc(one_used, 1)
                        dve.wait_ge(one_used, 3 * k + 3)
                dve.engine_nop().then_inc(rowmax_done, 1)

            def guard_out(n):
                dve.wait_ge(guard_psum, n + 1)
                dve.tensor_scalar(g_neg[:, :], ps[0:HEADS, TURN, :], -1.0, None, ALU.mult).then_inc(guard_read, 1)

            def guard_rest(n):
                dve.wait_ge(g_hi_done, n + 1)
                dve.tensor_tensor(g_res[:, :], g_neg[:, :], g_parts[:, 0, :], ALU.subtract).then_inc(g_res_done, 1)

            def guard_third(n):
                dve.wait_ge(g_mid_done, n + 1)
                dve.tensor_tensor(g_parts[:, 2, :], g_res[:, :], g_parts[:, 1, :],
                                  ALU.subtract).then_inc(guard_done, 1)

            def finish_group(b, t):
                g, cols = b * NG + t, slice(HG * HD * t, HG * HD * (t + 1))
                dve.wait_ge(sums_turned, g + 1)
                src = ps[:, TURN, :].rearrange("p (i h v) -> p i h v", i=NT, v=VW)
                dve.reciprocal(rden[:, :, :], src[:, :, :, HD]).then_inc(den_chain, 1)
                dve.wait_ge(den_chain, 2 * g + 1)
                dve.tensor_tensor(att[:, :, :, :], src[:, :, :, 0:HD],
                                  rden[:, :, :].unsqueeze(3).to_broadcast([P, NT, HG, HD]),
                                  ALU.mult).then_inc(att_done, 1)
                dve.wait_ge(att_done, g + 1)
                dve.tensor_tensor(att_step[:, :, :], att[:, :, :, :].rearrange("p i h d -> p i (h d)"),
                                  rows(0, b)[:, :, cols], ALU.mult).then_inc(den_chain, 1)
                dve.wait_ge(den_chain, 2 * g + 2)
                apart(dve, based, b + 1)
                dve.tensor_tensor(xt[:, b, :, cols], xt[:, b, :, cols], att_step[:, :, :],
                                  ALU.add).then_inc(x2_done, 1)

            def second_moments(n):
                apart(dve, x2_done, (n + 1) * NG)
                res_c.start(dve, n)
                moments(res_c, xt[:, n], stats2, mv2, nr2, seeded2)

            def second_ln(n):
                dve.wait_ge(rstd2_done, n + 1)
                after(dve, h2_turned, n)
                normalise(xs2, xt[:, n], mv2, nr2, xs2_done)
                res_c.end()

            def wide(t_, n_=E):
                return t_.unsqueeze(2).to_broadcast([P, NT, n_])

            def router(n):
                dve.wait_ge(logits, n + 1)
                gate_c.start(dve, n)
                lp = ps[:, TURN, 0:NT * E].rearrange("p (i e) -> p i e", e=E)
                dve.tensor_tensor(lgt[:, :, :], lp, rb[:, :].unsqueeze(1).to_broadcast([P, NT, E]),
                                  ALU.add).then_inc(logits_read, 1)
                dve.wait_ge(logits_read, n + 1)
                gate_c.link(dve.tensor_reduce(lmx[:, :], lgt[:, :, :], AX_X, ALU.max))
                dve.tensor_tensor(lgt[:, :, :], lgt[:, :, :], wide(lmx[:, :]), ALU.subtract).then_inc(lgt_done, 1)

            def router_gates(n):
                dve.wait_ge(pex_done, n + 1)
                gate_c.link(dve.tensor_reduce(pz[:, 0, :], pex[:, :, :], AX_X, ALU.add))
                gate_c.link(dve.reciprocal(pz[:, 1, :], pz[:, 0, :]))
                gate_c.link(dve.tensor_tensor(prb[:, :, 0:E], pex[:, :, :], wide(pz[:, 1, :]), ALU.mult), alone=True)
                for i in range(NT):
                    ins = dve.max(top8[:, i, :], prb[:, i, 0:E])
                gate_c.link(ins)
                gate_c.link(dve.tensor_copy(top8[:, :, TOPK:8], prb[:, :, E:E + 2]), alone=True)
                for i in range(NT):
                    ins = dve.match_replace(rest[:, i, :], top8[:, i, :], prb[:, i, :], 0.0)
                gate_c.link(ins)
                gate_c.link(dve.tensor_tensor(gsel[:, :, :], prb[:, :, 0:E], rest[:, :, 0:E], ALU.subtract))
                gate_c.link(dve.tensor_reduce(pz[:, 2, :], gsel[:, :, :], AX_X, ALU.add))
                gate_c.link(dve.tensor_scalar(pz[:, 2, :], pz[:, 2, :], FFN_EPS, None, ALU.add))
                gate_c.link(dve.reciprocal(pz[:, 3, :], pz[:, 2, :]))
                gate_c.link(dve.tensor_tensor(gate[:, :, :], gsel[:, :, :], wide(pz[:, 3, :]), ALU.mult))
                gate_c.link(dve.tensor_reduce(pz[:, 4, :], gate[:, :, :], AX_X, ALU.add))
                dve.tensor_scalar(eps_of[other(n)][:, :], pz[:, 4, :], FFN_EPS, None, ALU.mult)
                gate_c.link(dve.tensor_scalar(pz[:, 5, :], pz[:, 4, :], FFN_EPS, None, ALU.max))
                gate_c.link(dve.reciprocal(pz[:, 0, :], pz[:, 5, :]))
                gate_c.link(dve.scalar_tensor_tensor(gate_of[other(n)][:, :, :], gate[:, :, :], scal[:, 3:4],
                                                     wide(pz[:, 0, :]), ALU.mult, ALU.mult))
                gate_c.end()

            def experts(n, q):
                i, cc = divmod(q, CPT)
                k = i * (CPT - 1) + cc - 1
                dve.wait_ge(expert, n * CHUNKS + q + 1)
                if cc:
                    after(dve, added, n * NT * (CPT - 1) + k - 1)
                dst = gated[:, k % 2] if cc else acc[:, i]
                src = ps[:, EXPERT + q % 2, :].rearrange("p (e d) -> p e d", d=D)
                g = gate_of[other(n)][:, i, CE * cc:CE * cc + CE].unsqueeze(2).to_broadcast([P, CE, D])
                dve.tensor_tensor(dst, src, g, ALU.mult).then_inc(expert_used, 1)

            def finish_sums(n):
                dve.wait_ge(added, (n + 1) * NT * (CPT - 1))
                fin_c.start(dve, n)
                fin_c.link(dve.tensor_tensor(acc2[:, :, :, :], acc[:, :, 0:2, :], acc[:, :, 2:4, :], ALU.add))
                for i in range(NT):
                    ins = dve.scalar_tensor_tensor(ffn_row[:, i, :], acc2[:, i, 0, :], eps_of[1][:, i:i + 1],
                                                   acc2[:, i, 1, :], ALU.add, ALU.add)
                fin_c.link(ins)

            def finish(n):
                fin_c.link(dve.tensor_tensor(ffn_step[:, :, :], ffn_row[:, :, :], rows(2, n), ALU.mult))
                dve.tensor_tensor(xt[:, n], xt[:, n], ffn_step[:, :, :], ALU.add).then_inc(y_done, 1)
                dve.wait_ge(y_done, n + 1)
                fin_c.end()

            dve.memset(own[:, :, :], 0.0).then_inc(dve_chain, 1)
            dve.memset(prb[:, :, E:E + 1], -1.0).then_inc(dve_chain, 1)
            dve.memset(prb[:, :, E + 1:E + 2], -2.0).then_inc(dve_chain, 1)
            n_setup[0] = 3
            dve.memset(qry[:, :, :, :, :].bitcast(F32), 0.0).then_inc(zeroed, 1)
            dve.wait_ge(dve_chain, 3)
            for i in range(NT):
                dve.memset(own[0:RB, i, 2 * i:2 * i + 1], 1.0)
                ins = dve.memset(own[RB:P, i, 2 * i + 1:2 * i + 2], 1.0)
            link(ins)
            dve.wait_ge(act_set, 1)
            link(dve.tensor_scalar(c_exp[:, :], c_exp[:, :], 1.0, None, ALU.add))
            link(dve.reciprocal(c_exp[:, :], c_exp[:, :]))
            dve.tensor_tensor(c_in[:, :], c_in[:, :], c_exp[:, :], ALU.mult).then_inc(dve_set, 1)
            dve.wait_ge(x0_in, 32)
            prep_ln(0)
            dve.wait_ge(pe_set, 1)
            dve.tensor_copy(siluT[:, :], ps[:, TURN, 0:B]).then_inc(dve_set, 1)
            newton(dve, Chain(nwt_chain), 0, nr, seeded, rstd_done)
            prep_xs(0)
            dve.wait_ge(pe_set, 2)
            link(dve.tensor_copy(modT[:, :, :], ps[:, EXPERT, 0:6 * B].rearrange("p (k b) -> p k b", b=B)))
            dve.tensor_scalar(modT[:, 4, :], modT[:, 4, :], 1.0, None, ALU.add).then_inc(dve_chain, 1)
            dve.tensor_scalar(modT[:, 1, :], modT[:, 1, :], 1.0, None, ALU.add).then_inc(dve_chain, 1)
            n_setup[0] += 2
            dve.wait_ge(dve_chain, n_setup[0])
            dve.engine_nop().then_inc(dve_set, 2)
            dve.wait_ge(act_set, 2)
            link(dve.tensor_scalar(wcol[:, 1:2], wcol[:, 1:2], 1.0, None, ALU.add))
            link(dve.reciprocal(wcol[:, 2:3], wcol[:, 1:2]))
            link(dve.tensor_scalar(wcol[:, 3:4], wcol[:, 2:3], -1.0, 1.0, ALU.mult, ALU.add))
            link(dve.tensor_scalar(mask_w[:, :, :], own[:, :, :], wcol[:, 3:4], wcol[:, 2:3], ALU.mult, ALU.add))
            dve.tensor_reduce(bound[:, 0:1], modT[:, 1, :], AX_X, ALU.max, apply_absolute_value=True)
            dve.tensor_reduce(bound[:, 1:2], modT[:, 0, :], AX_X, ALU.max,
                              apply_absolute_value=True).then_inc(dve_set, 1)
            scale_h(0)
            dve.wait_ge(pe_set, 3)
            link(dve.tensor_copy(rwT[:, :], ps[:, EXPERT + 1, 2 * P:2 * P + E]))
            link(dve.tensor_reduce(bound1[:, 0:2], ps[0:1, EXPERT + 1, 0:2 * P].rearrange("p (k n) -> p k n", k=2),
                                   AX_X, ALU.max))
            link(dve.tensor_scalar(bound1[:, 2:3], bound1[:, 0:1], float(D) ** 0.5, None, ALU.mult))
            link(dve.scalar_tensor_tensor(bound1[:, 3:4], bound1[:, 1:2], float(HD) ** 0.5, bound1[:, 2:3],
                                          ALU.mult, ALU.add))
            dve.tensor_scalar(unsafe[:, :], bound1[:, 3:4], bound1[:, 3:4], float(SAFE_NORM2), ALU.mult,
                              ALU.is_gt).then_inc(flag_set, 1)
            first_rest(0)
            third_parts(0)
            dve.wait_ge(flag_set, 1)
            unsafe_v = dve.value_load(unsafe[0:1, 0:1], min_val=0, max_val=1)

            def guard(n):
                with dve.If(unsafe_v):
                    true_max(n)

            guard(0)
            guard_out(0)
            guard_rest(0)
            guard_third(0)
            dve.wait_ge(x1_in, 32)

            n_ext = [0]

            def link_ext(ins):
                n_ext[0] += 1
                ins.then_inc(ext_set, 1)
                dve.wait_ge(ext_set, n_ext[0])

            def extents():
                dve.wait_ge(we_in, 16)
                dve.tensor_reduce(extent[:, 0:1], we[:, :, :].rearrange("p e d -> p (e d)"), AX_X, ALU.max,
                                  apply_absolute_value=True)
                dve.tensor_reduce(extent[:, 1:2], modT[:, 4, :], AX_X, ALU.max, apply_absolute_value=True)
                link_ext(dve.tensor_reduce(extent[:, 2:3], modT[:, 3, :], AX_X, ALU.max, apply_absolute_value=True))

            def scales():
                dve.wait_ge(ext_turned, 1)
                link_ext(dve.tensor_reduce(ext1[:, 0:3], ps[0:1, EXPERT, 0:3 * P].rearrange("p (k n) -> p k n", k=3),
                                           AX_X, ALU.max))
                dve.tensor_scalar(ext1[:, 5:6], ext1[:, 0:1], 2.0 ** -40, None, ALU.max)
                link_ext(dve.scalar_tensor_tensor(ext1[:, 4:5], ext1[:, 1:2], float(D) ** 0.5, ext1[:, 2:3], ALU.mult,
                                                  ALU.add))
                link_ext(dve.tensor_scalar(ext1[:, 4:5], ext1[:, 4:5], 2.0 ** -40, None, ALU.max))
                link_ext(dve.tensor_scalar(ext_exp[:, :], ext1[:, 4:6].bitcast(I32), 23, None, ALU.arith_shift_right))
                step = float(1 << 23)
                dve.tensor_scalar(scal1[:, 4:6].bitcast(I32), ext_exp[:, :], step, -TOP * step, ALU.mult, ALU.add)
                dve.tensor_scalar(scal1[:, 0:2].bitcast(I32), ext_exp[:, :], -step, (254 + TOP) * step, ALU.mult,
                                  ALU.add).then_inc(ext_inv, 1)
                dve.wait_ge(ext_inv, 1)
                dve.tensor_scalar(scal1[:, 2:3], scal1[:, 4:5], 1.0, None, ALU.mult)
                link_ext(dve.tensor_tensor(scal1[:, 3:4], scal1[:, 4:5], scal1[:, 5:6], ALU.mult))

            def scale_rows():
                dve.wait_ge(ext_turned, 2)
                link_ext(dve.tensor_copy(scal[:, :], ps[:, EXPERT, 0:4]))
                dve.tensor_scalar(modT[:, 3:5, :], modT[:, 3:5, :], scal[:, 0:1], None, ALU.mult)
                link_ext(dve.tensor_scalar(rwT[:, :], rwT[:, :], scal[:, 2:3], None, ALU.mult))

            def split_h2(n):
                dve.wait_ge(h2_hi_done, n + 1)
                parts_ = h2_parts_of[other(n)]
                dve.tensor_tensor(parts_[:, 1, :], h2_of[other(n)][:, :], parts_[:, 0, :],
                                  ALU.subtract).then_inc(h2_split, 1)

            def body(b, tail, head, prep):
                for s in range(16):
                    t, hh = divmod(s, HG)
                    first = isinstance(b, int) and b * NG + t < 1
                    if isinstance(b, int) and b == 0 and s == 5:
                        dve.wait_ge(act_set, 8)
                        dve.wait_ge(rows_done, 6)
                    if hh == 2 and not first:
                        finish_group(b if t else b - 1, (t - 1) % NG)
                    if s == 0 and prep:
                        prep_ln(b + 1)
                    if s == 5 and prep:
                        prep_xs(b + 1)
                    if s == 7 and head:
                        second_moments(b - 1)
                    if s == 8 and prep:
                        scale_h(b + 1)
                        guard(b + 1)
                    if s == 9 and prep:
                        guard_out(b + 1)
                        first_rest(b + 1)
                    if s == 9 and head:
                        second_ln(b - 1)
                    if s == 10 and prep:
                        third_parts(b + 1)
                    if s == 11 and prep:
                        guard_rest(b + 1)
                    if s == 11 and tail:
                        finish_sums(b - 2)
                    if s == 12 and head:
                        router(b - 1)
                        split_h2(b - 1)
                    if s == 12 and prep:
                        guard_third(b + 1)
                    if s == 13 and head:
                        router_gates(b - 1)
                    if tail:
                        for q in tail_chunks[s]:
                            experts(b - 2, q)
                    if head:
                        for q in (head_chunks if prep else last_head_chunks)[s]:
                            experts(b - 1, q)
                    if s == 15 and tail:
                        finish(b - 2)
                    if s == 8 and isinstance(b, int) and b == 0:
                        extents()
                    if s == 10 and isinstance(b, int) and b == 0:
                        scales()
                    if s == 12 and isinstance(b, int) and b == 0:
                        scale_rows()
                    if s == 2 and isinstance(b, int) and b == 1:
                        dve.wait_ge(we_hi_done, 1)
                        dve.scalar_tensor_tensor(we_parts[:, 1].rearrange("p e d -> p (e d)"),
                                                 we[:, :, :].rearrange("p e d -> p (e d)"), scal[:, 1:2],
                                                 we_parts[:, 0].rearrange("p e d -> p (e d)"), ALU.mult,
                                                 ALU.subtract)
                    if s == 15 and isinstance(b, int) and b == 0:
                        dve.wait_ge(x_in, 32 * (B - 2))
                        dve.wait_ge(rb_in, 16)

            schedule(dve, body)
            def drain_chunk(n, q):
                i, cc = divmod(q, CPT)
                dve.wait_ge(expert, n * CHUNKS + q + 1)
                dst = acc[:, i] if n == B - 2 and cc == 0 else drain_w(n)[:, i, cc]
                src = ps[:, drain_bank(n, q), :].rearrange("p (e d) -> p e d", d=D)
                g = gate_of[other(n)][:, i, CE * cc:CE * cc + CE].unsqueeze(2).to_broadcast([P, CE, D])
                dve.tensor_tensor(dst, src, g, ALU.mult).then_inc(drain_vec, 1)

            nwt2 = Chain(nwt2_chain, per=11)
            finish_group(B - 1, NG - 1)
            second_moments(B - 1)
            newton(dve, nwt2, B - 1, nr2, seeded2, rstd2_done)
            second_ln(B - 1)
            for q in DRAIN_VEC:
                drain_chunk(B - 2, q)
            dve.wait_ge(h2_done, B)
            dve.tensor_copy(h2_parts_of[0][:, 0, :], h2_of[0][:, :]).then_inc(h2_hi_done, 1)
            split_h2(B - 1)
            router(B - 1)
            router_gates(B - 1)

            n_last = [0]

            def link_last(ins):
                n_last[0] += 1
                ins.then_inc(last_chain, 1)
                dve.wait_ge(last_chain, n_last[0])

            def finish_tile(i):
                for k in (2 * i, 2 * i + 1):
                    if k in VEC_PAIRS:
                        cc = 2 * (k % 2)
                        wait_drained(dve, B - 1, 2 * k)
                        wait_drained(dve, B - 1, 2 * k + 1)
                        link_last(dve.tensor_tensor(last_w[:, i, cc], last_w[:, i, cc], last_w[:, i, cc + 1], ALU.add))
                by_pool = sum(k not in VEC_PAIRS for k in range(2 * i + 2))
                if by_pool:
                    dve.wait_ge(last_pair, by_pool)
                link_last(dve.tensor_tensor(last_w[:, i, 1], last_w[:, i, 0], last_w[:, i, 2], ALU.add))
                link_last(dve.tensor_tensor(last_w[:, i, 3, 0:2], last_w[:, i, 1, 0:2], last_w[:, i, 1, 2:4], ALU.add))
                link_last(dve.scalar_tensor_tensor(last_w[:, i, 3, 2], last_w[:, i, 3, 0], eps_of[0][:, i:i + 1],
                                                   last_w[:, i, 3, 1], ALU.add, ALU.add))
                link_last(dve.tensor_tensor(last_w[:, i, 3, 3], last_w[:, i, 3, 2], gate_rows[:, 2, B - 1, :], ALU.mult))
                dve.tensor_tensor(xt[:, B - 1, i], xt[:, B - 1, i], last_w[:, i, 3, 3], ALU.add).then_inc(last_y, 1)

            for i in range(NT):
                for q in range(CPT * i, CPT * (i + 1)):
                    if drain_on_vec(B - 1, q):
                        drain_chunk(B - 1, q)
                if i:
                    finish_tile(i - 1)
            finish_tile(NT - 1)

        @block.tensor
        def _(pe):
            mm = pe.matmul

            def turn4(src, done):
                for i in range(NT):
                    ins = pe.transpose(ps[:, TURN, i * P:(i + 1) * P], src(i), ident[:, :])
                ins.then_inc(done, 1)

            def prep_turn(n):
                pe.wait_ge(xs_done, n + 1)
                turn4(lambda i: xs[:, i, :], hT_turned)

            def prep_guard(n):
                with pe.If(unsafe_v):
                    with pe.Fori(0, HEADS) as h:
                        pe.wait_ge(one_done, n * HEADS + h + 1)
                        for i in range(NT):
                            k = n * HEADS * NT + h * NT + i
                            if i:
                                pe.wait_ge(one_used, 3 * k)
                            mm(ps[:, EXPERT + 1, :], h_one[:, i * P:(i + 1) * P], h3[:, 0, :], start=True,
                               stop=True).then_inc(one_score, 1)
                    pe.wait_ge(rowmax_done, n + 1)
                    for i in range(NT):
                        ins = pe.transpose(ps[0:HEADS, TURN, i * P:(i + 1) * P], rowmax[:, i, :], ident[:, :])
                    ins.then_inc(guard_psum, 1)
                with pe.Else():
                    pe.wait_ge(sq_done, n + 1)
                    mm(ps[0:HEADS, TURN, :], head_sel[:, :], sq[:, :], start=True,
                       stop=True).then_inc(guard_psum, 1)

            def scores(b, t, i):
                if i == 0:
                    pe.wait_ge(loaded[t % 2], (b * 2 + t // 2 + 1) * 6 * 16)
                lo, sl = i * P, t % 2
                for j in range(2):
                    after(pe, expd, b * BU + t * UNITS + 2 * i + j - 1)
                    for half in range(2):
                        rows_ = slice(half * (P // 2), (half + 1) * (P // 2))
                        mm(ps[:, 2 * j + half, :], keys[rows_, sl, j, lo:lo + P], qry[rows_, sl, j, 0, :],
                           start=True, stop=False, skip_group_check=True)
                    for r in range(2):
                        at = lo + r * RB
                        for half in range(2):
                            rows_ = slice(half * (P // 2), (half + 1) * (P // 2))
                            ins = mm(ps[r * RB:(r + 1) * RB, 2 * j + half, at:at + RB], keys[rows_, sl, j, at:at + RB],
                                     qry[rows_, sl, j, 1, at:at + RB], start=False, stop=True, skip_group_check=True)
                    ins.then_inc(scored, 1)

            def sums(g, t, i):
                if i == 0:
                    pe.wait_ge(vals_done, g + 1)
                    after(pe, sums_out, g)
                pe.wait_ge(expd, g * UNITS + 2 * i + 2)
                for hh in range(HG):
                    ins = mm(ps[VW * hh:VW * hh + VW, SUMS, :], vals[:, i, HG * t + hh, :],
                             probs[:, t % 2, hh, i, :], start=(i == 0), stop=(i == NT - 1), skip_group_check=True)
                if i == NT - 1:
                    ins.then_inc(summed, 1)

            def sums_turn(g):
                pe.wait_ge(sums_out, g + 1)
                turn4(lambda i: o_sb[:, i * P:(i + 1) * P], sums_turned)

            def h2_turn(n):
                pe.wait_ge(xs2_done, n + 1)
                turn4(lambda i: xs2[:, i, :], h2_turned)

            def route(n):
                pe.wait_ge(h2_done, n + 1)
                for i in range(NT):
                    ins = mm(ps[:, TURN, i * E:(i + 1) * E], h2_of[other(n)][:, i * P:(i + 1) * P], rwT[:, :], start=True, stop=True)
                ins.then_inc(logits, 1)

            def expert_product(bank, n, i, cc):
                for k, (hp, wp) in enumerate(EXPERT_PARTS):
                    ins = mm(ps[:, bank, :], h2_parts_of[other(n)][:, hp, i * P:(i + 1) * P],
                             we_parts[:, wp, CE * cc:CE * cc + CE, :], start=(k == 0),
                             stop=(k == len(EXPERT_PARTS) - 1))
                ins.then_inc(expert, 1)

            def experts(n, q):
                i, cc = divmod(q, CPT)
                if q == 0:
                    pe.wait_ge(h2_split, n + 1)
                after(pe, expert_used, n * CHUNKS + q - 1)
                expert_product(EXPERT + q % 2, n, i, cc)

            pe.wait_ge(pool_set, 4)
            pe.wait_ge(dve_set, 1)
            pe.transpose(ps[:, TURN, 0:B], c_in[:, :], ident[0:B, 0:B]).then_inc(pe_set, 1)
            pe.wait_ge(consts_in, 16)
            pe.wait_ge(dve_set, 2)
            for k in range(6):
                ins = mm(ps[:, EXPERT, k * B:(k + 1) * B], wmod_sb[:, k * D:(k + 1) * D], siluT[:, :],
                         start=True, stop=True)
            ins.then_inc(pe_set, 1)
            prep_turn(0)
            pe.wait_ge(small_in, 32)
            pe.transpose(ps[:, EXPERT + 1, 2 * P:2 * P + E], rw_in[:, :], ident[0:E, 0:E])
            pe.wait_ge(dve_set, 5)
            for k in range(2):
                ins = pe.transpose(ps[0:1, EXPERT + 1, k * P:(k + 1) * P], bound[:, k:k + 1], ident[:, :])
            ins.then_inc(pe_set, 1)
            pe.wait_ge(flag_set, 1)
            unsafe_v = pe.value_load(unsafe[0:1, 0:1], min_val=0, max_val=1)
            pe.wait_ge(hT_done, 1)
            pe.wait_ge(pool_set, 6)
            prep_guard(0)

            def chunks(b, s, tail, head, prep):
                if tail:
                    for q in tail_chunks[s]:
                        experts(b - 2, q)
                if head:
                    for q in (head_chunks if prep else last_head_chunks)[s]:
                        experts(b - 1, q)

            def gate_row(n):
                pe.wait_ge(diag_set, n + 1)
                after(pe, act_set, 2 + n - 1)
                mm(ps[:, EXPERT + n % 2, :], ones[:, :], acc[:, n % NT, :, :], start=True,
                   stop=True).then_inc(rows_done, 1)

            for n in range(ROWS_EARLY):
                gate_row(n)
            pe.wait_ge(zeroed, 1)
            pe.wait_ge(pool_set, 9)

            def body(b, tail, head, prep):
                for s in range(16):
                    t, hh = divmod(s, HG)
                    g = b * NG + t
                    scores(b, t, hh)
                    if isinstance(b, int) and b == 0:
                        for n in GATE_ROWS.get(s, ()):
                            gate_row(n)
                    first_experts = s in (4, 8, 10)
                    if first_experts:
                        chunks(b, s, tail, head, prep)
                    if hh:
                        sums(g, t, hh - 1)
                    elif not (isinstance(b, int) and g < 1):
                        sums(g - 1, (t - 1) % NG, NT - 1)
                    if hh == 1 and not (isinstance(b, int) and g < 1):
                        if t < 2:
                            after(pe, att_done, g - 1)
                        elif t == 2:
                            pe.wait_ge(guard_read, b + 2) if prep else pe.wait_ge(att_done, g - 1)
                        elif head:
                            pe.wait_ge(logits_read, b)
                        else:
                            pe.wait_ge(att_done, g - 1)
                        sums_turn(g - 1)
                    if s == 6 and prep:
                        pe.wait_ge(att_done, b * NG + 1)
                        prep_turn(b + 1)
                    if s == 8 and prep:
                        pe.wait_ge(hT_done, b + 2)
                        prep_guard(b + 1)
                    if s == 10 and head:
                        pe.wait_ge(att_done, b * NG + 2)
                        h2_turn(b - 1)
                    if s == 11 and head:
                        route(b - 1)
                    if not first_experts:
                        chunks(b, s, tail, head, prep)
                    if s == 9 and isinstance(b, int) and b == 0:
                        pe.wait_ge(ext_set, 1)
                        pe.wait_ge(act_set, 8)
                        for k in range(3):
                            ins = pe.transpose(ps[0:1, EXPERT, k * P:(k + 1) * P], extent[:, k:k + 1], ident[:, :])
                        ins.then_inc(ext_turned, 1)
                    if s == 11 and isinstance(b, int) and b == 0:
                        pe.wait_ge(ext_set, 6)
                        mm(ps[:, EXPERT, 0:4], ones[0:1, :], scal1[:, 0:4], start=True, stop=True).then_inc(ext_turned, 1)

            schedule(pe, body)
            last = B * NG - 1

            def drain_chunk(n, q):
                i, cc = divmod(q, CPT)
                at = DRAIN.index((n, q))
                if at == 0:
                    pe.wait_ge(expd, B * BU)
                if at < len(DRAIN_BANKS):
                    pe.wait_ge(expert_used, DRAIN[0][0] * CHUNKS + DRAIN[0][1])
                else:
                    wait_drained(pe, *DRAIN[at - len(DRAIN_BANKS)])
                expert_product(drain_bank(n, q), n, i, cc)

            rest_q = [q for n, q in DRAIN if n == B - 2]
            sums(last, NG - 1, 3)
            drain_chunk(B - 2, rest_q[0])
            pe.wait_ge(att_done, last)
            sums_turn(last)
            for q in rest_q[1:9]:
                drain_chunk(B - 2, q)
            pe.wait_ge(att_done, last + 1)
            h2_turn(B - 1)
            for q in rest_q[9:11]:
                drain_chunk(B - 2, q)
            route(B - 1)
            for q in rest_q[11:]:
                drain_chunk(B - 2, q)
            pe.wait_ge(h2_split, B)
            for q in range(CHUNKS):
                drain_chunk(B - 1, q)


_INS = ["L0_attn_x", "L0_attn_inter_palace_weight", "L0_ffn_router_w", "L0_ffn_router_b", "L0_ffn_expert_w",
        "L0_c", "L0_wmod"]


def kernel(**inputs):
    import concourse.bacc as _bacc
    from concourse.bass_utils import run_bass_kernel_spmd as _run

    nc = _bacc.Bacc("TRN2", target_bir_lowering=False, num_devices=1)
    arrays, args = {}, []
    for name in _INS:
        a = np.ascontiguousarray(inputs[name])
        a = a.reshape(a.shape or (1,))
        arrays[f"in_{name}_dram"] = a
        args.append(nc.dram_tensor(f"in_{name}_dram", a.shape, mybir.dt.from_np(a.dtype), kind="ExternalInput").ap())
    shape = inputs["L0_attn_x"].shape
    out = nc.dram_tensor("out_0_dram", shape, F32, kind="ExternalOutput").ap()
    adaln_block(nc, *args, out)
    r = _run(nc, [arrays], core_ids=[0])
    return r.results[0]["out_0_dram"]
```
